# Optimizing a Trainium2 kernel written in Bass

```python
import numpy as np
import jax
import jax.numpy as jnp

def _softmax(x, axis=-1):
    return jax.nn.softmax(x, axis=axis)

def _gelu(x):
    return jax.nn.gelu(x, approximate=True)

def _silu(x):
    return jax.nn.silu(x)

def _sigmoid(x):
    return jax.nn.sigmoid(x)

def _layernorm(x, axis=-1, eps=1e-05):
    m = jnp.mean(x, axis=axis, keepdims=True)
    v = jnp.var(x, axis=axis, keepdims=True)
    return (x - m) / jnp.sqrt(v + eps)

def _scatter_add(tgt, idx, src, axis=0):
    return tgt.at[idx].add(src)

def _segment_sum(src, seg, n):
    return jax.ops.segment_sum(src, seg, n)
kernel_name = 'mk_prb_d1_jaxref_r4_24a59b'

def setup_inputs(seed: int=0):
    np.random.seed(seed)
    _w = jnp.asarray

    def _L0_attn_setup():
        import jax, jax.numpy as jnp
        import numpy as np
        H = 16
        key = jax.random.key(seed)
        ks = jax.random.split(key, 7)
        B, L, D, d = (1, 256, 256, 256 // H)
        s = 0.02
        return {'x': jax.random.normal(ks[0], (B, L, D), jnp.float32), 'Wq': jax.random.normal(ks[1], (D, D), jnp.float32) * s, 'Wk': jax.random.normal(ks[2], (D, D), jnp.float32) * s, 'Wv': jax.random.normal(ks[3], (D, D), jnp.float32) * s, 'Wo': jax.random.normal(ks[4], (D, D), jnp.float32) * s, 'gw': jax.random.normal(ks[5], (1, d), jnp.float32) * s, 'sw': jax.random.normal(ks[6], (1, d), jnp.float32) * s}
    _L0_attn_in = _L0_attn_setup()

    def _L0_ffn_setup():
        import jax, jax.numpy as jnp
        import numpy as np

        def _bitlinear(x, w_latent):
            scale = jax.lax.stop_gradient(jnp.clip(jnp.mean(jnp.abs(w_latent), axis=1, keepdims=True), 1e-05, None))
            tern = jnp.clip(jnp.round(w_latent / scale), -1.0, 1.0)
            w = w_latent + jax.lax.stop_gradient(tern - w_latent)
            return x @ (w * scale).T
        key = jax.random.key(seed)
        ks = jax.random.split(key, 6)
        dim, hidden, rank = (256, 1024, 16)
        B, S = (4, 1024)
        x = jax.random.normal(ks[0], (B, S, dim), dtype=jnp.float32)
        w_fc = 0.02 * jax.random.normal(ks[1], (hidden, dim), dtype=jnp.float32)
        w_proj = 0.02 * jax.random.normal(ks[2], (dim, hidden), dtype=jnp.float32)
        u = 0.02 * jax.random.normal(ks[3], (hidden, rank), dtype=jnp.float32)
        v = 0.02 * jax.random.normal(ks[4], (rank, dim), dtype=jnp.float32)
        fast_b = jax.random.normal(ks[5], (rank, rank), dtype=jnp.float32)
        gate = jnp.float32(0.05)
        return {'x': x, 'fast_b': fast_b, 'w_fc': w_fc, 'w_proj': w_proj, 'u': u, 'v': v, 'gate': gate}
    _L0_ffn_in = _L0_ffn_setup()
    _d = {'L0_attn_x': _L0_attn_in['x'], 'L0_attn_Wq': _L0_attn_in['Wq'], 'L0_attn_Wk': _L0_attn_in['Wk'], 'L0_attn_Wv': _L0_attn_in['Wv'], 'L0_attn_Wo': _L0_attn_in['Wo'], 'L0_attn_gw': _L0_attn_in['gw'], 'L0_attn_sw': _L0_attn_in['sw'], 'L0_ffn_fast_b': _L0_ffn_in['fast_b'], 'L0_ffn_w_fc': _L0_ffn_in['w_fc'], 'L0_ffn_w_proj': _L0_ffn_in['w_proj'], 'L0_ffn_u': _L0_ffn_in['u'], 'L0_ffn_v': _L0_ffn_in['v'], 'L0_ffn_gate': _L0_ffn_in['gate']}
    _x0 = _d['L0_attn_x']
    _d['L0_attn_x'] = jax.random.normal(jax.random.fold_in(jax.random.key(seed), 1), (8, 1024, 256), dtype=_x0.dtype)
    del _x0
    return _d

def reference(L0_attn_x, L0_attn_Wq, L0_attn_Wk, L0_attn_Wv, L0_attn_Wo, L0_attn_gw, L0_attn_sw, L0_ffn_fast_b, L0_ffn_w_fc, L0_ffn_w_proj, L0_ffn_u, L0_ffn_v, L0_ffn_gate):

    def _L0_attn_ref(x, Wq, Wk, Wv, Wo, gw, sw):
        import jax, jax.numpy as jnp
        import numpy as np
        H = 16
        B, L, D = x.shape
        d = D // H
        Q = (x @ Wq.T).reshape(B, L, H, d)
        K = (x @ Wk.T).reshape(B, L, H, d)
        V = (x @ Wv.T).reshape(B, L, H, d)
        KV = jnp.einsum('blhd,blhe->blhde', K, V)
        g = jax.nn.sigmoid(x.reshape(B, L, H, d) @ gw.T)
        g = jnp.clip(g, 1e-06, None)
        log_c = jnp.clip(jnp.cumsum(jnp.log(g), axis=1), -30.0, 30.0)
        Gc = (jnp.exp(log_c) + 1e-06)[..., None]
        R = jax.nn.silu(K @ sw.T)[..., None]
        S = jnp.cumsum(KV * R / Gc, axis=1) * Gc
        out = jnp.einsum('blhd,blhde->blhe', Q, S).reshape(B, L, D)
        return out @ Wo.T

    def _L0_ffn_ref(x, fast_b, w_fc, w_proj, u, v, gate):
        import jax, jax.numpy as jnp
        import numpy as np

        def _bitlinear(x, w_latent):
            scale = jax.lax.stop_gradient(jnp.clip(jnp.mean(jnp.abs(w_latent), axis=1, keepdims=True), 1e-05, None))
            tern = jnp.clip(jnp.round(w_latent / scale), -1.0, 1.0)
            w = w_latent + jax.lax.stop_gradient(tern - w_latent)
            return x @ (w * scale).T
        h = _bitlinear(x, w_fc) + gate * (x @ v.T @ fast_b.T @ u.T)
        r = jnp.maximum(h, 0.0)
        return _bitlinear(r * r, w_proj)
    x = L0_attn_x
    xn = _layernorm(x, axis=-1)
    x = x + _L0_attn_ref(xn, L0_attn_Wq, L0_attn_Wk, L0_attn_Wv, L0_attn_Wo, L0_attn_gw, L0_attn_sw) + _L0_ffn_ref(xn, L0_ffn_fast_b, L0_ffn_w_fc, L0_ffn_w_proj, L0_ffn_u, L0_ffn_v, L0_ffn_gate)
    return x

_drawn_inputs = setup_inputs


def setup_inputs(seed=0):
    import zlib

    import numpy as np

    out = dict(_drawn_inputs(seed))
    spreads = {}
    factors = {'L0_attn_Wq': 4.262,
     'L0_attn_Wk': 4.38,
     'L0_attn_Wv': 4.216,
     'L0_attn_Wo': 4.226,
     'L0_attn_gw': 8.0,
     'L0_attn_sw': 4.544,
     'L0_ffn_fast_b': 8.0,
     'L0_ffn_u': 8.0,
     'L0_ffn_v': 8.0,
     'L0_ffn_w_fc': 8.0}
    for name, (base, spread) in spreads.items():
        noise = np.random.default_rng([zlib.crc32(name.encode()), seed]).standard_normal(out[name].shape)
        drawn = base * np.exp(spread * noise) if base else spread * noise
        out[name] = jnp.asarray(drawn.astype(out[name].dtype))
    for name, factor in factors.items():
        out[name] = (out[name] * factor).astype(out[name].dtype)
    return out
```

```python
from contextlib import ExitStack

import numpy as np

import concourse.bass as bass
from concourse import mybir

F32 = mybir.dt.float32
F32R = mybir.dt.float32r
F16 = mybir.dt.float16
I32 = mybir.dt.int32
ALU = mybir.AluOpType
ACT = mybir.ActivationFunctionType
AX = mybir.AxisListType

P = 128
B, L, D = 8, 1024, 256
H, HD = 16, 16
HID = 1024
RANK = 16
KT = D // P
HT = HID // P
UNIT = 256
CH = UNIT // P
NU = L // UNIT
PAIRS = H // 2
VG = D + 2 * H
WTOK = 2 * D + VG
EPS = 1e-5

(XT, QK0, VG0, QK1, VG1, KS0, CUM, QS0, QT, KS1, QS1, GCT) = range(12)
FILLS = 12
FRONT_A = (XT, VG0, VG1, CUM, QS0, QS1)


def unit_after(b, u, k):
    return b + (u + k) // NU, (u + k) % NU


def exists(b):
    return not isinstance(b, int) or 0 <= b < B


def upto(b, u, per_unit, k):
    return (b * NU + u) * per_unit + k + 1


def started(value):
    return not isinstance(value, int) or value > 0


def gated_attention_ternary_ffn(nc, x, wq_t, wk_t, wv_t, wo_t, wq, wk, gw, sw, fb_t, v, u_t, gate, w_fc, w_proj,
                                ident, causal, same_head, head_of, out):
    x_v = x.rearrange("b l d -> (b l) d").rearrange("(t c p) d -> t p c d", c=CH, p=P)
    out_v = out.rearrange("b l d -> (b l) d").rearrange("(t c p) d -> t p c d", c=CH, p=P)

    with ExitStack() as ctx:
        def sb(name, shape, dt=F32):
            return ctx.enter_context(nc.sbuf_tensor(name, shape, dt))

        def psum(name):
            return ctx.enter_context(nc.psum_tensor(name, [P, 512], F32))

        def sem(name):
            return ctx.enter_context(nc.semaphore(name))

        ident_sb = sb("ident_sb", [P, P])
        ident16 = sb("ident16", [P, P], F16)
        causal_sb = sb("causal_sb", [P, P])
        same_head_sb = sb("same_head_sb", [P, P])
        head_of_sb = sb("head_of_sb", [P, KT, H])
        ones = sb("ones", [P, P])
        w_stage = sb("w_stage", [P, KT, WTOK])
        wtok_h = sb("wtok_h", [P, KT, WTOK], F32R)
        wtok_l = sb("wtok_l", [P, KT, WTOK], F32R)
        wo_stage = sb("wo_stage", [P, KT, D])
        wo_h = sb("wo_h", [P, KT, D], F32R)
        wo_l = sb("wo_l", [P, KT, D], F32R)
        wfc_h = sb("wfc_h", [P, KT, HID], F32R)
        wfc_l = sb("wfc_l", [P, KT, HID], F32R)
        wproj_t = sb("wproj_t", [P, HT, D], F32R)
        proj_scale = sb("proj_scale", [P, D])
        unscale = sb("unscale", [P, H])
        row_max = sb("row_max", [P, 2, KT])
        head_pow = sb("head_pow", [P, 2, KT])
        head_inv = sb("head_inv", [P, 2, KT])
        head_un = sb("head_un", [P, KT])
        gw_col = sb("gw_col", [P, KT])
        sw_col = sb("sw_col", [P, KT])
        sw_diag = sb("sw_diag", [P, KT, H])
        fbt_sb = sb("fbt_sb", [RANK, RANK])
        v_sb = sb("v_sb", [RANK, D])
        ut_sb = sb("ut_sb", [RANK, HID])
        gate_sb = sb("gate_sb", [RANK, 1])
        fbv = sb("fbv", [RANK, D])
        fc_scale = sb("fc_scale", [P, 3, HT])
        pj_scale = sb("pj_scale", [P, 3, KT])
        inv_proj = sb("inv_proj", [P, D])
        x_sb = sb("x_sb", [P, NU, CH, D])
        stats = sb("stats", [P, CH, 6])
        moments = sb("moments", [P, 2, CH, 2])
        neg_mean = sb("neg_mean", [P, 2, CH])
        var_eps = sb("var_eps", [P, 2, CH])
        log_var = sb("log_var", [P, 2, CH])
        guess = sb("guess", [P, 2, CH])
        newton = sb("newton", [P, 2, CH, 2])
        rstd = sb("rstd", [P, 2, CH])
        xn = sb("xn", [P, 2, CH, D])
        xt_h = sb("xt_h", [P, NU, CH, KT, P], F32R)
        xt_l = sb("xt_l", [P, NU, CH, KT, P], F32R)
        qk = sb("qk", [P, 2, CH, 2 * D])
        vg = sb("vg", [P, 2, CH, VG])
        parts = sb("parts", [P, CH, 2 * H, 4, HD], F16)
        k_stack = sb("k_stack", [P, 2, CH, PAIRS, P], F16)
        q_diag = sb("q_diag", [P, 2, CH, PAIRS, 2, P], F16)
        q_t = sb("q_t", [P, 2, CH, KT, P])
        exp_neg = sb("exp_neg", [P, CH, 2 * H])
        gate_den = sb("gate_den", [P, CH, H])
        write_den = sb("write_den", [P, CH, H])
        log_den = sb("log_den", [P, CH, H])
        before = sb("before", [P, 2, CH, H])
        log_c = sb("log_c", [P, CH, H])
        decay = sb("decay", [P, CH, H])
        write_full = sb("write_full", [P, CH, H])
        write_rec = sb("write_rec", [P, CH, H])
        write = sb("write", [P, 2, CH, H])
        decay_out = sb("decay_out", [P, CH, H])
        decay_rep = sb("decay_rep", [P, CH, D])
        decay_t = sb("decay_t", [P, 2, CH, KT, P])
        v_pad = sb("v_pad", [P, 2, CH, H, 2 * HD])
        masked = sb("masked", [P, 4, 512])
        state = sb("state", [P, KT, P])
        state_diag = sb("state_diag", [P, KT, P])
        attn = sb("attn", [P, CH, KT, P])
        attn_h = sb("attn_h", [P, 2, CH, KT, P], F32R)
        attn_l = sb("attn_l", [P, 2, CH, KT, P], F32R)
        relu_sq = sb("relu_sq", [P, 4, 512])
        relu, sq = relu_sq[:, 0:2], relu_sq[:, 2:4]
        sq_h = sb("sq_h", [P, 4, 512], F32R)
        sq_l = sb("sq_l", [P, 4, 512], F32R)
        y_both = sb("y_both", [P, 4, CH, D])
        y_scaled, y_out = y_both[:, 0:2], y_both[:, 2:4]
        fc_nat = masked[:].rearrange("p g n -> p (g n)").rearrange("p (t n) -> p t n", t=HT)
        pj_nat = relu_sq[:].rearrange("p g n -> p (g n)").rearrange("p (t n) -> p t n", t=KT)
        qk_nat = y_both[:, 0:2]
        below = y_both[:].rearrange("p g c n -> p (g c n)")

        front_a = psum("front_a")
        front_b = psum("front_b")
        score_bank = [psum("score_a"), psum("score_b")]
        attn_bank = psum("attn_bank")
        hid_bank = [psum("hid_a"), psum("hid_b")]
        y_bank = psum("y_bank")

        x_loaded = [sem(f"x_loaded{i}") for i in range(NU)]
        attn_weights_loaded = sem("attn_weights_loaded")
        ffn_weights_loaded = sem("ffn_weights_loaded")
        zeroed = sem("zeroed")
        setup_v = sem("setup_v")
        setup_pe = sem("setup_pe")
        stats_done = sem("stats_done")
        moments_done = sem("moments_done")
        ln_ready = sem("ln_ready")
        log_var_done = sem("log_var_done")
        guess_done = sem("guess_done")
        newton_step = sem("newton_step")
        rstd_done = sem("rstd_done")
        xn_done = sem("xn_done")
        front_full = sem("front_full")
        xt_h_done = sem("xt_h_done")
        xt_l_done = sem("xt_l_done")
        qk_done = sem("qk_done")
        vg_done = sem("vg_done")
        part_h_done = sem("part_h_done")
        part_l_done = sem("part_l_done")
        parts_done = sem("parts_done")
        k_stack_done = sem("k_stack_done")
        q_diag_done = sem("q_diag_done")
        q_t_done = sem("q_t_done")
        exp_neg_done = sem("exp_neg_done")
        dens_done = sem("dens_done")
        log_den_done = sem("log_den_done")
        before_step = sem("before_step")
        log_c_done = sem("log_c_done")
        decay_done = sem("decay_done")
        write_step = sem("write_step")
        write_done = sem("write_done")
        decay_out_done = sem("decay_out_done")
        decay_rep_done = sem("decay_rep_done")
        decay_t_done = sem("decay_t_done")
        v_pad_done = sem("v_pad_done")
        score_full = sem("score_full")
        mask_done = sem("mask_done")
        values_done = sem("values_done")
        attn_full = sem("attn_full")
        attn_done = sem("attn_done")
        state_done = sem("state_done")
        state_diag_done = sem("state_diag_done")
        attn_h_done = sem("attn_h_done")
        attn_l_done = sem("attn_l_done")
        hid_full = sem("hid_full")
        relu_done = sem("relu_done")
        sq_done = sem("sq_done")
        sq_h_done = sem("sq_h_done")
        sq_l_done = sem("sq_l_done")
        proj_done = sem("proj_done")
        y_full = sem("y_full")
        y_scaled_done = sem("y_scaled_done")
        y_out_done = sem("y_out_done")
        stored = [sem("stored_even"), sem("stored_odd")]

        ATTN_LOADS, FFN_LOADS = 16, 2
        V_ROW_MAX, V_HEAD_SCALES, V_SW_DIAG, V_SMALL_READ, V_WTOK, V_TERNARY, V_FC_READ, V_DONE = (
            1, 5, 6, 12, 14, 25, 33, 42)
        PE_HEAD_SUM, PE_SMALL, PE_FC, PE_PROJ, PE_ROW = 1, 2, 3, 4, 5

        def heads_bc(ap, n):
            return ap.unsqueeze(len(ap.shape)).to_broadcast([*ap.shape, n])

        def v_heads(par, c, first, count):
            flat = v_pad[:, par, c].rearrange("p h x -> p (h x)")[:, first * 2 * HD:(first + count) * 2 * HD]
            return flat.rearrange("p (g s e) -> p g s e", s=4, e=HD)[:, :, 0:4:3, :]

        block = ctx.enter_context(nc.Block())

        @block.sync
        def _(sp):
            def load(b, u):
                if not exists(b):
                    return
                if started(upto(b, u, 1, 0) - NU):
                    sp.wait_ge(y_out_done, upto(b, u, 1, 0) - NU)
                sp.dma_start(x_sb[:, u], x_v[b * NU + u]).then_inc(x_loaded[u], 16)

            def store(b, u):
                if not exists(b):
                    return
                sp.wait_ge(y_out_done, upto(b, u, 1, 0))
                sp.dma_start(out_v[b * NU + u], y_out[:, u % 2]).then_inc(stored[u % 2], 16)

            def slot(b, u):
                load(*unit_after(b, u, 3))
                store(*unit_after(b, u, -1))

            load(0, 0)
            small = [(ident_sb[:], ident), (causal_sb[:], causal), (same_head_sb[:], same_head),
                     (head_of_sb[:], head_of.rearrange("(t p) h -> p t h", p=P)),
                     (qk_nat[:, 0], wq.rearrange("(t p) n -> p t n", p=P)),
                     (qk_nat[:, 1], wk.rearrange("(t p) n -> p t n", p=P)),
                     (w_stage[:, :, 0:D], wq_t.rearrange("(t p) n -> p t n", p=P)),
                     (w_stage[:, :, D:2 * D], wk_t.rearrange("(t p) n -> p t n", p=P)),
                     (w_stage[:, :, 2 * D:3 * D], wv_t.rearrange("(t p) n -> p t n", p=P)),
                     (wo_stage[:], wo_t.rearrange("(t p) n -> p t n", p=P)),
                     (gw_col[:], gw), (sw_col[:], sw),
                     (fbt_sb[:], fb_t), (v_sb[:], v), (ut_sb[:], u_t), (gate_sb[:], gate)]
            assert len(small) == ATTN_LOADS
            for dst, src in small:
                sp.dma_start(dst, src).then_inc(attn_weights_loaded, 16)
            sp.dma_start(fc_nat, w_fc.rearrange("(t p) n -> p t n", p=P)).then_inc(ffn_weights_loaded, 16)
            sp.dma_start(pj_nat, w_proj.rearrange("(t p) n -> p t n", p=P)).then_inc(ffn_weights_loaded, 16)
            load(0, 1)
            load(0, 2)
            for u in range(NU):
                slot(0, u)
            with sp.Fori(1, B - 1) as b:
                for u in range(NU):
                    slot(b, u)
            for u in range(NU):
                slot(B - 1, u)
            slot(B, 0)
            for par in range(2):
                sp.wait_ge(stored[par], 16 * B * NU // 2)

        @block.gpsimd
        def _(pool):
            def waits_to_normalise(b, u):
                if not exists(b):
                    return
                pool.wait_ge(rstd_done, upto(b, u, 1, 0))
                if started(upto(b, u, FILLS, XT) - 2 * FILLS):
                    pool.wait_ge(front_full, upto(b, u, FILLS, XT) - 2 * FILLS)

            def normalise(b, u):
                if not exists(b):
                    return
                for c in range(CH):
                    nc.gpsimd.tensor_scalar(xn[:, u % 2, c], x_sb[:, u, c], neg_mean[:, u % 2, c:c + 1],
                                            rstd[:, u % 2, c:c + 1], ALU.add, ALU.mult).then_inc(xn_done, 1)

            def values_and_decay(b, u):
                if not exists(b):
                    return
                par = u % 2
                pool.wait_ge(write_done, upto(b, u, 1, 0))
                pool.wait_ge(vg_done, upto(b, u, CH, CH - 1))
                pb, pu = unit_after(b, u, -2)
                if exists(pb):
                    pool.wait_ge(attn_full, upto(pb, pu, CH, CH - 1))
                for c in range(CH):
                    if c == CH - 1:
                        pool.wait_ge(decay_out_done, upto(b, u, 1, 0))
                        if started(upto(b, u, FILLS, GCT) - FILLS):
                            pool.wait_ge(front_full, upto(b, u, FILLS, GCT) - FILLS)
                    val = vg[:, par, c, 0:D].rearrange("p (g s e) -> p g s e", s=2, e=HD)
                    fac = heads_bc(write[:, par, c], HD).rearrange("p (g s) e -> p g s e", s=2)
                    nc.gpsimd.tensor_tensor(v_heads(par, c, 0, H), val, fac, ALU.mult).then_inc(v_pad_done, 1)
                nc.gpsimd.tensor_scalar(decay_rep[:].rearrange("p c (h e) -> p (c h) e", e=HD),
                                        heads_bc(decay_out[:].rearrange("p c h -> p (c h)"), HD), 1.0, 1.0,
                                        ALU.mult, ALU.mult).then_inc(decay_rep_done, 1)

            def diagonal_state(b, u, c):
                if not exists(b):
                    return
                pool.wait_ge(state_done, upto(b, u, CH, c))
                if (u, c) != (NU - 1, CH - 1):
                    nc.gpsimd.tensor_tensor(state_diag[:], state[:],
                                            same_head_sb[:].unsqueeze(1).to_broadcast([P, KT, P]),
                                            ALU.mult).then_inc(state_diag_done, 1)

            def attn_parts(b, u, c):
                if not exists(b):
                    return
                pb, pu = unit_after(b, u, -2)
                if exists(pb):
                    pool.wait_ge(y_full, upto(pb, pu, 1, 0))
                pool.wait_ge(attn_done, upto(b, u, CH, c))
                nc.gpsimd.tensor_tensor(attn_h[:, u % 2, c], attn[:, c], ones[:].unsqueeze(1).to_broadcast([P, KT, P]),
                                        ALU.mult).then_inc(attn_h_done, 1)
                pool.wait_ge(attn_h_done, upto(b, u, CH, c))
                nc.gpsimd.tensor_tensor(attn_l[:, u % 2, c], attn[:, c], attn_h[:, u % 2, c].bitcast(F32),
                                        ALU.subtract).then_inc(attn_l_done, 1)
                if (u, c) == (NU - 1, CH - 1):
                    nc.gpsimd.memset(state_diag[:], 0.0).then_inc(state_diag_done, 1)

            def residual(b, u):
                if not exists(b):
                    return
                pool.wait_ge(y_scaled_done, upto(b, u, 1, 0))
                pb, pu = unit_after(b, u, -2)
                if exists(pb):
                    pool.wait_ge(stored[u % 2], (pb * (NU // 2) + pu // 2 + 1) * 16)
                nc.gpsimd.tensor_tensor(y_out[:, u % 2], y_scaled[:, u % 2], x_sb[:, u], ALU.add).then_inc(y_out_done, 1)

            def slot(b, u):
                nxt, prev, after = unit_after(b, u, 1), unit_after(b, u, -1), unit_after(b, u, 2)
                diagonal_state(b, u, 0)
                attn_parts(b, u, 0)
                waits_to_normalise(*after)
                values_and_decay(*nxt)
                normalise(*after)
                diagonal_state(b, u, 1)
                attn_parts(b, u, 1)
                residual(*prev)

            nc.gpsimd.memset(v_pad[:], 0.0).then_inc(zeroed, 1)
            nc.gpsimd.memset(q_diag[:], 0.0).then_inc(zeroed, 1)
            nc.gpsimd.memset(ones[:], 1.0).then_inc(zeroed, 1)
            nc.gpsimd.memset(state_diag[:], 0.0).then_inc(zeroed, 1)
            waits_to_normalise(0, 0)
            normalise(0, 0)
            pool.wait_ge(zeroed, 4)
            slot(-1, NU - 1)
            for u in range(NU):
                slot(0, u)
            with pool.Fori(1, B - 1) as b:
                for u in range(NU):
                    slot(b, u)
            for u in range(NU):
                slot(B - 1, u)
            slot(B, 0)

        @block.scalar
        def _(act):
            def filled(b, u, fill):
                act.wait_ge(front_full, upto(b, u, FILLS, fill))
                return front_a if fill in FRONT_A else front_b

            def rstd_guess(b, u):
                if not exists(b):
                    return
                par = u % 2
                act.wait_ge(ln_ready, upto(b, u, 1, 0))
                nc.scalar.activation(log_var[:, par], var_eps[:, par], ACT.Ln).then_inc(log_var_done, 1)
                act.wait_ge(log_var_done, upto(b, u, 1, 0))
                nc.scalar.activation(guess[:, par], log_var[:, par], ACT.Exp, scale=-0.5).then_inc(guess_done, 1)

            def xt_high(b, u):
                if not exists(b):
                    return
                bank = filled(b, u, XT)
                pb, pu = unit_after(b, u, -NU)
                if exists(pb):
                    act.wait_ge(hid_full, upto(pb, pu, 4, 3))
                nc.scalar.activation(xt_h[:, u], bank[:].rearrange("p (c t n) -> p c t n", c=CH, t=KT),
                                     ACT.Copy).then_inc(xt_h_done, 1)

            def projected(b, u, c):
                if not exists(b):
                    return
                par = u % 2
                bank = filled(b, u, [QK0, QK1][c])
                pb, pu = unit_after(b, u, -2)
                if exists(pb):
                    act.wait_ge(attn_full, upto(pb, pu, CH, CH - 1))
                    act.wait_ge(v_pad_done, upto(pb, pu, CH, CH - 1))
                nc.scalar.activation(qk[:, par, c], bank[:], ACT.Copy).then_inc(qk_done, 1)
                pb, pu = unit_after(b, u, -1)
                if exists(pb):
                    act.wait_ge(front_full, upto(pb, pu, FILLS, QS1))
                nc.scalar.activation(parts[:, c, :, 0, :], bank[:].rearrange("p (h e) -> p h e", e=HD),
                                     ACT.Copy).then_inc(part_h_done, 1)
                bank = filled(b, u, [VG0, VG1][c])
                nc.scalar.activation(vg[:, par, c], bank[:, 0:VG], ACT.Copy).then_inc(vg_done, 1)

            def gate_exp(b, u):
                if not exists(b):
                    return
                act.wait_ge(vg_done, upto(b, u, CH, CH - 1))
                pb, pu = unit_after(b, u, -1)
                if exists(pb):
                    act.wait_ge(dens_done, upto(pb, pu, 2, 1))
                nc.scalar.activation(exp_neg[:], vg[:, u % 2, :, D:VG], ACT.Exp, scale=-1.0).then_inc(exp_neg_done, 1)

            def gate_log(b, u):
                if not exists(b):
                    return
                act.wait_ge(dens_done, upto(b, u, 2, 1))
                pb, pu = unit_after(b, u, -1)
                if exists(pb):
                    act.wait_ge(front_full, upto(pb, pu, FILLS, CUM))
                    act.wait_ge(before_step, upto(pb, pu, 2, 1))
                nc.scalar.activation(log_den[:], gate_den[:], ACT.Ln).then_inc(log_den_done, 1)

            def keys_stacked(b, u, c):
                if not exists(b):
                    return
                bank = filled(b, u, [KS0, KS1][c])
                pb, pu = unit_after(b, u, -2)
                if exists(pb):
                    act.wait_ge(score_full, upto(pb, pu, 4 * CH, 4 * CH - 1))
                nc.scalar.activation(k_stack[:, u % 2, c], bank[:].bitcast(F16).rearrange("p (g n) -> p g n", g=PAIRS),
                                     ACT.Copy).then_inc(k_stack_done, 1)

            def queries_stacked(b, u, c):
                if not exists(b):
                    return
                bank = filled(b, u, [QS0, QS1][c])
                if isinstance(b, int) and b == 0 and u < 2:
                    act.wait_ge(zeroed, 4)
                for half in range(2):
                    rows = slice(64 * half, 64 * half + 64)
                    nc.scalar.activation(q_diag[rows, u % 2, c, :, half, :],
                                         bank[rows].bitcast(F16).rearrange("p (g n) -> p g n", g=PAIRS),
                                         ACT.Copy).then_inc(q_diag_done, 1)

            def query_t(b, u):
                if not exists(b):
                    return
                bank = filled(b, u, QT)
                nc.scalar.activation(q_t[:, u % 2], bank[:].rearrange("p (c t n) -> p c t n", c=CH, t=KT),
                                     ACT.Copy).then_inc(q_t_done, 1)

            def decay_exp(b, u):
                if not exists(b):
                    return
                act.wait_ge(log_c_done, upto(b, u, 1, 0))
                pb, pu = unit_after(b, u, -1)
                if exists(pb):
                    act.wait_ge(decay_out_done, upto(pb, pu, 1, 0))
                nc.scalar.activation(decay[:], log_c[:], ACT.Exp, scale=-1.0).then_inc(decay_done, 1)

            def decay_transposed(b, u):
                if not exists(b):
                    return
                bank = filled(b, u, GCT)
                pb, pu = unit_after(b, u, -2)
                if exists(pb):
                    act.wait_ge(attn_done, upto(pb, pu, CH, CH - 1))
                nc.scalar.activation(decay_t[:, u % 2], bank[:].rearrange("p (c t n) -> p c t n", c=CH, t=KT),
                                     ACT.Copy).then_inc(decay_t_done, 1)

            def squares(b, u, q):
                if not exists(b):
                    return
                n = q % 2
                act.wait_ge(hid_full, upto(b, u, 4, q))
                nc.scalar.activation(relu[:, n], hid_bank[n][:], ACT.Relu).then_inc(relu_done, 1)
                if started(upto(b, u, 4, q) - 2):
                    act.wait_ge(sq_l_done, upto(b, u, 4, q) - 2)
                act.wait_ge(relu_done, upto(b, u, 4, q))
                nc.scalar.activation(sq[:, n], relu[:, n], ACT.Square).then_inc(sq_done, 1)

            def slot(b, u):
                nxt, prev, after = unit_after(b, u, 1), unit_after(b, u, -1), unit_after(b, u, 2)
                projected(*nxt, 0)
                squares(*prev, 0)
                projected(*nxt, 1)
                gate_exp(*nxt)
                gate_log(*nxt)
                squares(*prev, 1)
                keys_stacked(*nxt, 0)
                squares(*prev, 2)
                rstd_guess(*after)
                decay_exp(*nxt)
                queries_stacked(*nxt, 0)
                query_t(*nxt)
                squares(*prev, 3)
                keys_stacked(*nxt, 1)
                queries_stacked(*nxt, 1)
                decay_transposed(*nxt)
                xt_high(*after)

            nc.scalar.preload_act_table_set("natural_log_exp_and_others")
            rstd_guess(0, 0)
            xt_high(0, 0)
            slot(-1, NU - 1)
            for u in range(NU):
                slot(0, u)
            with act.Fori(1, B - 1) as b:
                for u in range(NU):
                    slot(b, u)
            for u in range(NU):
                slot(B - 1, u)
            slot(B, 0)

        @block.vector
        def _(dve):
            steps = [0]

            def step(ins):
                steps[0] += 1
                ins.then_inc(setup_v, 1)
                dve.wait_ge(setup_v, steps[0])

            def head_scales():
                step(nc.vector.tensor_reduce(row_max[:].rearrange("p w t -> p (w t)"),
                                             qk_nat.rearrange("p w t n -> p (w t) n"), AX.X, ALU.max,
                                             apply_absolute_value=True))
                assert steps[0] == V_ROW_MAX
                dve.wait_ge(setup_pe, PE_HEAD_SUM)
                pow2 = head_pow[:].rearrange("p w t -> p (w t)")
                step(nc.vector.tensor_scalar(pow2, score_bank[0][:, 0:2 * KT], 1e-30, None, ALU.max))
                step(nc.vector.tensor_scalar(pow2.bitcast(I32), pow2.bitcast(I32), 0x7F800000, None, ALU.bitwise_and))
                step(nc.vector.reciprocal(head_inv[:].rearrange("p w t -> p (w t)"), pow2))
                step(nc.vector.tensor_tensor(head_un[:], head_pow[:, 0], head_pow[:, 1], ALU.mult))
                assert steps[0] == V_HEAD_SCALES

            def token_weights():
                nc.vector.tensor_scalar(sw_diag[:, 0], head_of_sb[:, 0], sw_col[:, 0:1], None, ALU.mult)
                step(nc.vector.tensor_scalar(sw_diag[:, 1], head_of_sb[:, 1], sw_col[:, 1:2], None, ALU.mult))
                assert steps[0] == V_SW_DIAG
                dve.wait_ge(setup_pe, PE_SMALL)
                for t in range(KT):
                    cols = w_stage[:, t, 0:2 * D]
                    step(nc.vector.tensor_tensor(cols, cols, hid_bank[0][:], ALU.mult))
                nc.vector.tensor_scalar(w_stage[:, 0, 3 * D:3 * D + H], head_of_sb[:, 0], gw_col[:, 0:1], None, ALU.mult)
                nc.vector.tensor_scalar(w_stage[:, 1, 3 * D:3 * D + H], head_of_sb[:, 1], gw_col[:, 1:2], None, ALU.mult)
                step(nc.vector.tensor_copy(w_stage[:, :, 3 * D + H:WTOK],
                                           hid_bank[1][:, 0:KT * H].rearrange("p (t h) -> p t h", t=KT)))
                step(nc.vector.tensor_scalar(unscale[:], score_bank[1][:, 0:H], 1.0 / HD, None, ALU.mult))
                step(nc.vector.tensor_copy(fbv[:], score_bank[0][0:RANK, 0:D]))
                step(nc.vector.tensor_scalar(ut_sb[:], ut_sb[:], gate_sb[:, 0:1], None, ALU.mult))
                assert steps[0] == V_SMALL_READ
                step(nc.vector.tensor_copy(wtok_h[:], w_stage[:]))
                step(nc.vector.tensor_tensor(wtok_l[:], w_stage[:], wtok_h[:].bitcast(F32), ALU.subtract))
                assert steps[0] == V_WTOK

            def ternary(nat, tiles, width, scales):
                step(nc.vector.tensor_reduce(scales[:, 0], nat, AX.X, ALU.add, apply_absolute_value=True))
                step(nc.vector.tensor_scalar(scales[:, 0], scales[:, 0], 1.0 / width, 1e-5, ALU.mult, ALU.max))
                nc.vector.tensor_scalar(scales[:, 1], scales[:, 0], 0.5, None, ALU.mult)
                step(nc.vector.tensor_scalar(scales[:, 2], scales[:, 0], -0.5, None, ALU.mult))
                low = below.rearrange("p (t n) -> p t n", t=tiles)
                for t in range(tiles):
                    last = nc.vector.tensor_scalar(low[:, t], nat[:, t], scales[:, 2, t:t + 1], None, ALU.is_lt)
                step(last)
                for t in range(tiles):
                    last = nc.vector.scalar_tensor_tensor(out=nat[:, t], in0=nat[:, t], scalar=scales[:, 1, t:t + 1],
                                                          in1=low[:, t], op0=ALU.is_gt, op1=ALU.subtract)
                return last

            def ffn_weights():
                last = ternary(fc_nat, HT, D, fc_scale)
                step(last)
                for t in range(HT):
                    last = nc.vector.tensor_scalar(fc_nat[:, t], fc_nat[:, t], fc_scale[:, 0, t:t + 1], None, ALU.mult)
                last.then_inc(setup_v, 1)
                steps[0] += 1
                dve.wait_ge(setup_v, steps[0])
                last = ternary(pj_nat, KT, HID, pj_scale)
                steps[0] += 1
                last.then_inc(setup_v, 1)
                dve.wait_ge(setup_v, steps[0])
                assert steps[0] == V_TERNARY
                dve.wait_ge(setup_pe, PE_FC)
                for i, bank in enumerate([front_a, front_b, attn_bank, y_bank]):
                    t, g = i // 2, i % 2
                    cols = slice(512 * g, 512 * g + 512)
                    step(nc.vector.tensor_copy(wfc_h[:, t, cols], bank[:]))
                    step(nc.vector.tensor_tensor(wfc_l[:, t, cols], bank[:], wfc_h[:, t, cols].bitcast(F32), ALU.subtract))
                assert steps[0] == V_FC_READ
                dve.wait_ge(setup_pe, PE_PROJ)
                for i, bank in enumerate([*score_bank, *hid_bank]):
                    last = nc.vector.tensor_copy(wproj_t[:, 2 * i:2 * i + 2, :],
                                                 bank[:].rearrange("p (t n) -> p t n", t=2))
                    step(last)
                dve.wait_ge(setup_pe, PE_ROW)
                step(nc.vector.tensor_copy(proj_scale[:], front_a[:, 0:D]))
                step(nc.vector.reciprocal(inv_proj[:], proj_scale[:]))
                step(nc.vector.tensor_tensor(wo_stage[:], wo_stage[:], inv_proj[:].unsqueeze(1).to_broadcast([P, KT, D]),
                                             ALU.mult))
                step(nc.vector.tensor_copy(wo_h[:], wo_stage[:]))
                step(nc.vector.tensor_tensor(wo_l[:], wo_stage[:], wo_h[:].bitcast(F32), ALU.subtract))
                assert steps[0] == V_DONE

            def stats_of(b, u):
                if not exists(b):
                    return
                dve.wait_ge(x_loaded[u], (b + 1) * 16)
                for c in range(CH):
                    last = nc.vector.bn_stats(stats[:, c], x_sb[:, u, c])
                last.then_inc(stats_done, 1)

            def waits_for_stats(b, u):
                if not exists(b):
                    return
                dve.wait_ge(stats_done, upto(b, u, 1, 0))

            def moments_of(b, u):
                if not exists(b):
                    return
                for c in range(CH):
                    last = nc.vector.bn_aggr(moments[:, u % 2, c], stats[:, c])
                last.then_inc(moments_done, 1)

            def scalars_of(b, u):
                if not exists(b):
                    return
                par = u % 2
                pb, pu = unit_after(b, u, -2)
                if exists(pb):
                    dve.wait_ge(xn_done, upto(pb, pu, CH, CH - 1))
                dve.wait_ge(moments_done, upto(b, u, 1, 0))
                nc.vector.tensor_scalar(neg_mean[:, par], moments[:, par, :, 0], -1.0, None, ALU.mult)
                nc.vector.tensor_scalar(var_eps[:, par], moments[:, par, :, 1], EPS, None, ALU.add).then_inc(ln_ready, 1)

            def refine_rstd(b, u):
                if not exists(b):
                    return
                par = u % 2
                y, a = guess[:, par], var_eps[:, par]
                sqr, corr = newton[:, par, :, 0], newton[:, par, :, 1]
                dve.wait_ge(guess_done, upto(b, u, 1, 0))
                dve.wait_ge(ln_ready, upto(b, u, 1, 0))
                nc.vector.tensor_tensor(sqr, y, y, ALU.mult).then_inc(newton_step, 1)
                dve.wait_ge(newton_step, upto(b, u, 2, 0))
                nc.vector.scalar_tensor_tensor(out=corr, in0=sqr, scalar=-0.5, in1=a, op0=ALU.mult,
                                               op1=ALU.mult).then_inc(newton_step, 1)
                dve.wait_ge(newton_step, upto(b, u, 2, 1))
                nc.vector.scalar_tensor_tensor(out=rstd[:, par], in0=corr, scalar=1.5, in1=y, op0=ALU.add,
                                               op1=ALU.mult).then_inc(rstd_done, 1)

            def xt_low(b, u):
                if not exists(b):
                    return
                dve.wait_ge(xt_h_done, upto(b, u, 1, 0))
                nc.vector.tensor_tensor(xt_l[:, u], front_a[:].rearrange("p (c t n) -> p c t n", c=CH, t=KT),
                                        xt_h[:, u].bitcast(F32), ALU.subtract).then_inc(xt_l_done, 1)

            def qk_parts(b, u, c):
                if not exists(b):
                    return
                src = qk[:, u % 2, c].rearrange("p (h e) -> p h e", e=HD)
                dve.wait_ge(part_h_done, upto(b, u, CH, c))
                nc.vector.tensor_tensor(parts[:, c, :, 2, :], src, parts[:, c, :, 0, :],
                                        ALU.subtract).then_inc(part_l_done, 1)
                dve.wait_ge(part_l_done, upto(b, u, CH, c))
                q, k = parts[:, c, 0:H], parts[:, c, H:2 * H]
                nc.vector.tensor_copy(q[:, :, 1::2, :], q[:, :, 0::2, :])
                nc.vector.tensor_copy(k[:, :, 3, :], k[:, :, 0, :])
                nc.vector.tensor_copy(k[:, :, 1, :], k[:, :, 2, :]).then_inc(parts_done, 1)

            def dens(b, u):
                if not exists(b):
                    return
                dve.wait_ge(exp_neg_done, upto(b, u, 1, 0))
                pb, pu = unit_after(b, u, -1)
                if exists(pb):
                    dve.wait_ge(log_den_done, upto(pb, pu, 1, 0))
                nc.vector.tensor_scalar(gate_den[:], exp_neg[:, :, 0:H], 1.0, 1e6, ALU.add, ALU.min).then_inc(dens_done, 1)
                nc.vector.tensor_scalar(write_den[:], exp_neg[:, :, H:2 * H], 1.0, None, ALU.add).then_inc(dens_done, 1)

            def sums_before(b, u):
                if not exists(b):
                    return
                par = u % 2
                dve.wait_ge(log_den_done, upto(b, u, 1, 0))
                if started(upto(b, u, 2, 0) - 1):
                    dve.wait_ge(before_step, upto(b, u, 2, 0) - 1)
                nc.vector.tensor_tensor(before[:, par, 1], before[:, par, 0], log_den[:, 0], ALU.add).then_inc(before_step, 1)
                dve.wait_ge(before_step, upto(b, u, 2, 0))
                if u == NU - 1:
                    nc.vector.memset(before[:, 1 - par, 0], 0.0).then_inc(before_step, 1)
                else:
                    nc.vector.tensor_tensor(before[:, 1 - par, 0], before[:, par, 1], log_den[:, 1],
                                            ALU.add).then_inc(before_step, 1)

            def clip_log(b, u):
                if not exists(b):
                    return
                dve.wait_ge(front_full, upto(b, u, FILLS, CUM))
                pb, pu = unit_after(b, u, -1)
                if exists(pb):
                    dve.wait_ge(decay_done, upto(pb, pu, 1, 0))
                nc.vector.tensor_scalar(log_c[:], front_a[:, 0:CH * H].rearrange("p (c h) -> p c h", c=CH), 30.0, -30.0,
                                        ALU.min, ALU.max).then_inc(log_c_done, 1)

            def decays(b, u):
                if not exists(b):
                    return
                par = u % 2
                dve.wait_ge(decay_done, upto(b, u, 1, 0))
                nc.vector.scalar_tensor_tensor(out=write_full[:], in0=decay[:], scalar=1e-6, in1=write_den[:],
                                               op0=ALU.add, op1=ALU.mult).then_inc(write_step, 1)
                dve.wait_ge(write_step, upto(b, u, 2, 0))
                nc.vector.reciprocal(write_rec[:], write_full[:]).then_inc(write_step, 1)
                pb, pu = unit_after(b, u, -2)
                if exists(pb):
                    dve.wait_ge(v_pad_done, upto(pb, pu, CH, CH - 1))
                dve.wait_ge(write_step, upto(b, u, 2, 1))
                nc.vector.tensor_tensor(write[:, par], write_rec[:], vg[:, par, :, D + H:VG], ALU.mult).then_inc(write_done, 1)
                pb, pu = unit_after(b, u, -1)
                if exists(pb):
                    dve.wait_ge(decay_rep_done, upto(pb, pu, 1, 0))
                nc.vector.scalar_tensor_tensor(out=decay_out[:], in0=decay[:], scalar=1e-6,
                                               in1=unscale[:].unsqueeze(1).to_broadcast([P, CH, H]),
                                               op0=ALU.add, op1=ALU.mult).then_inc(decay_out_done, 1)

            def mask(b, u, c, g):
                if not exists(b):
                    return
                dve.wait_ge(score_full, upto(b, u, 4 * CH, 4 * c + g))
                if started(upto(b, u, 2 * CH, 2 * c + g // 2) - 2):
                    dve.wait_ge(values_done, upto(b, u, 2 * CH, 2 * c + g // 2) - 2)
                nc.vector.tensor_tensor(masked[:, g].rearrange("p (h n) -> p h n", h=4),
                                        score_bank[g % 2][:].rearrange("p (h n) -> p h n", h=4),
                                        causal_sb[:].unsqueeze(1).to_broadcast([P, 4, P]), ALU.mult).then_inc(mask_done, 1)

            def chunk_out(b, u, c):
                if not exists(b):
                    return
                par = u % 2
                dve.wait_ge(attn_full, upto(b, u, CH, c))
                update = attn_bank[:, 2 * P:4 * P].rearrange("p (t n) -> p t n", t=KT)
                if started(upto(b, u, CH, c) - 1):
                    dve.wait_ge(state_diag_done, upto(b, u, CH, c) - 1)
                if (u, c) == (0, 0):
                    nc.vector.tensor_copy(state[:], update).then_inc(state_done, 1)
                else:
                    if started(upto(b, u, CH, c) - 1):
                        dve.wait_ge(state_done, upto(b, u, CH, c) - 1)
                    nc.vector.tensor_tensor(state[:], state[:], update, ALU.add).then_inc(state_done, 1)
                dve.wait_ge(decay_t_done, upto(b, u, 1, 0))
                pb, pu = unit_after(b, u, -1)
                if exists(pb):
                    dve.wait_ge(attn_l_done, upto(pb, pu, CH, c))
                nc.vector.tensor_tensor(attn[:, c], attn_bank[:, 0:2 * P].rearrange("p (t n) -> p t n", t=KT),
                                        decay_t[:, par, c], ALU.mult).then_inc(attn_done, 1)

            def split_squares(b, u, q):
                if not exists(b):
                    return
                n = q % 2
                dve.wait_ge(sq_done, upto(b, u, 4, q))
                if started(upto(b, u, 4, q) - 4):
                    dve.wait_ge(proj_done, upto(b, u, 4, q) - 4)
                nc.vector.tensor_copy(sq_h[:, q], sq[:, n]).then_inc(sq_h_done, 1)
                dve.wait_ge(sq_h_done, upto(b, u, 4, q))
                nc.vector.tensor_tensor(sq_l[:, q], sq[:, n], sq_h[:, q].bitcast(F32), ALU.subtract).then_inc(sq_l_done, 1)

            def scale_y(b, u):
                if not exists(b):
                    return
                dve.wait_ge(y_full, upto(b, u, 1, 0))
                pb, pu = unit_after(b, u, -2)
                if exists(pb):
                    dve.wait_ge(y_out_done, upto(pb, pu, 1, 0))
                nc.vector.tensor_tensor(y_scaled[:, u % 2], y_bank[:].rearrange("p (c n) -> p c n", c=CH),
                                        proj_scale[:].unsqueeze(1).to_broadcast([P, CH, D]),
                                        ALU.mult).then_inc(y_scaled_done, 1)

            def slot(b, u):
                nxt, prev, after = unit_after(b, u, 1), unit_after(b, u, -1), unit_after(b, u, 2)
                mask(b, u, 0, 0)
                mask(b, u, 0, 1)
                mask(b, u, 0, 2)
                mask(b, u, 0, 3)
                qk_parts(*nxt, 0)
                stats_of(*after)
                split_squares(*prev, 0)
                qk_parts(*nxt, 1)
                dens(*nxt)
                chunk_out(b, u, 0)
                waits_for_stats(*after)
                mask(b, u, 1, 0)
                moments_of(*after)
                mask(b, u, 1, 1)
                scalars_of(*after)
                sums_before(*nxt)
                split_squares(*prev, 1)
                mask(b, u, 1, 2)
                mask(b, u, 1, 3)
                clip_log(*nxt)
                split_squares(*prev, 2)
                refine_rstd(*after)
                decays(*nxt)
                chunk_out(b, u, 1)
                split_squares(*prev, 3)
                xt_low(*after)
                scale_y(*prev)

            nc.vector.memset(before[:], 0.0)
            stats_of(0, 0)
            waits_for_stats(0, 0)
            moments_of(0, 0)
            scalars_of(0, 0)
            refine_rstd(0, 0)
            dve.wait_ge(attn_weights_loaded, 16 * ATTN_LOADS)
            nc.vector.tensor_copy(ident16[:], ident_sb[:])
            head_scales()
            token_weights()
            dve.wait_ge(ffn_weights_loaded, 16 * FFN_LOADS)
            ffn_weights()
            xt_low(0, 0)
            slot(-1, NU - 1)
            for u in range(NU):
                slot(0, u)
            with dve.Fori(1, B - 1) as b:
                for u in range(NU):
                    slot(b, u)
            for u in range(NU):
                slot(B - 1, u)
            slot(B, 0)

        @block.tensor
        def _(pe):
            mm = nc.tensor.matmul

            def setup():
                pe.wait_ge(setup_v, V_ROW_MAX)
                mm(score_bank[0][:, 0:2 * KT], same_head_sb[:], row_max[:].rearrange("p w t -> p (w t)"),
                   start=True, stop=True).then_inc(setup_pe, 1)
                pe.wait_ge(setup_v, V_SW_DIAG)
                for i in range(2 * KT):
                    col = head_inv[:, i // KT, i % KT:i % KT + 1]
                    mm(hid_bank[0][:, i * P:i * P + P], col.to_broadcast([P, P]), ident_sb[:], start=True, stop=True)
                for m in range(KT):
                    for t in range(KT):
                        mm(hid_bank[1][:, m * H:m * H + H], qk_nat[:, 1, t, m * P:m * P + P], sw_diag[:, t],
                           start=(t == 0), stop=(t == KT - 1))
                for t in range(KT):
                    mm(score_bank[1][:, 0:H], head_un[:, t:t + 1].to_broadcast([P, P]), head_of_sb[:, t],
                       start=(t == 0), stop=(t == KT - 1))
                mm(score_bank[0][0:RANK, 0:D], fbt_sb[:], v_sb[:], start=True, stop=True).then_inc(setup_pe, 1)
                pe.wait_ge(setup_v, V_TERNARY)
                for i, bank in enumerate([front_a, front_b, attn_bank, y_bank]):
                    t, g = i // 2, i % 2
                    for j in range(4):
                        mm(bank[:, j * P:j * P + P], fc_nat[:, 4 * g + j, t * P:t * P + P], ident_sb[:],
                           start=(j == 0), stop=False, skip_group_check=True)
                    last = mm(bank[:], fbv[:, t * P:t * P + P], ut_sb[:, 512 * g:512 * g + 512],
                              start=False, stop=True, skip_group_check=True)
                last.then_inc(setup_pe, 1)
                for i, bank in enumerate([*score_bank, *hid_bank]):
                    for j in range(2):
                        for o in range(KT):
                            last = nc.tensor.transpose(bank[:, j * D + o * P:j * D + o * P + P],
                                                       pj_nat[:, o, (2 * i + j) * P:(2 * i + j) * P + P], ident_sb[:])
                last.then_inc(setup_pe, 1)
                pe.wait_ge(setup_v, V_FC_READ)
                for o in range(KT):
                    last = mm(front_a[:, o * P:o * P + P], pj_scale[:, 0, o:o + 1].to_broadcast([P, P]), ident_sb[:],
                              start=True, stop=True)
                last.then_inc(setup_pe, 1)
                pe.wait_ge(setup_v, V_DONE)

            def tokens_t(b, u):
                if not exists(b):
                    return
                pb, pu = unit_after(b, u, -1)
                if exists(pb):
                    pe.wait_ge(q_diag_done, upto(pb, pu, 2 * CH, 3))
                for c in range(CH):
                    pe.wait_ge(xn_done, upto(b, u, CH, c))
                    for t in range(KT):
                        at = (c * KT + t) * P
                        last = nc.tensor.transpose(front_a[:, at:at + P], xn[:, u % 2, c, t * P:t * P + P], ident_sb[:])
                last.then_inc(front_full, 1)

            def token_product(bank, u, c, cols, width):
                n = 0
                for t in range(KT):
                    for lhs, rhs in ((xt_h, wtok_h), (xt_h, wtok_l), (xt_l, wtok_h)):
                        last = mm(bank[:, 0:width], lhs[:, u, c, t], rhs[:, t, cols:cols + width],
                                  start=(n == 0), stop=(n == 3 * KT - 1))
                        n += 1
                return last

            def project(b, u, c):
                if not exists(b):
                    return
                pe.wait_ge(xt_l_done, upto(b, u, 1, 0))
                if c == 0:
                    pb, pu = unit_after(b, u, -1)
                    if exists(pb):
                        pe.wait_ge(decay_t_done, upto(pb, pu, 1, 0))
                else:
                    pe.wait_ge(part_h_done, upto(b, u, CH, 0))
                token_product(front_b, u, c, 0, 2 * D).then_inc(front_full, 1)
                if c == 1:
                    pe.wait_ge(vg_done, upto(b, u, CH, 0))
                token_product(front_a, u, c, 2 * D, VG).then_inc(front_full, 1)

            def stack_keys(b, u, c):
                if not exists(b):
                    return
                bank = front_b[:].bitcast(F16)
                pe.wait_ge(parts_done, upto(b, u, CH, c))
                if c == 0:
                    pe.wait_ge(part_h_done, upto(b, u, CH, 1))
                else:
                    pe.wait_ge(q_t_done, upto(b, u, 1, 0))
                for g in range(PAIRS):
                    last = nc.tensor.transpose(bank[:, g * P:g * P + P],
                                               parts[:, c, H + 2 * g:H + 2 * g + 2].rearrange("p h s e -> p (h s e)"),
                                               ident16[:])
                last.then_inc(front_full, 1)

            def stack_queries(b, u, c):
                if not exists(b):
                    return
                bank = front_a[:].bitcast(F16)
                if c == 0:
                    pe.wait_ge(log_c_done, upto(b, u, 1, 0))
                else:
                    pe.wait_ge(q_diag_done, upto(b, u, 2 * CH, 1))
                for g in range(PAIRS):
                    last = nc.tensor.transpose(bank[:, g * P:g * P + P],
                                               parts[:, c, 2 * g:2 * g + 2].rearrange("p h s e -> p (h s e)"),
                                               ident16[:])
                last.then_inc(front_full, 1)

            def queries_t(b, u):
                if not exists(b):
                    return
                pe.wait_ge(k_stack_done, upto(b, u, CH, 0))
                for c in range(CH):
                    for t in range(KT):
                        at = (c * KT + t) * P
                        last = nc.tensor.transpose(front_b[:, at:at + P], qk[:, u % 2, c, t * P:t * P + P], ident_sb[:])
                last.then_inc(front_full, 1)

            def cumulate(b, u):
                if not exists(b):
                    return
                pe.wait_ge(vg_done, upto(b, u, CH, 1))
                pe.wait_ge(before_step, upto(b, u, 2, 0))
                cum = front_a[:, 0:CH * H]
                mm(cum, causal_sb[:], log_den[:].rearrange("p c h -> p (c h)"), start=True, stop=False)
                mm(cum, ones[:], before[:, u % 2].rearrange("p c h -> p (c h)"),
                   start=False, stop=True).then_inc(front_full, 1)

            def decay_rows(b, u):
                if not exists(b):
                    return
                pe.wait_ge(k_stack_done, upto(b, u, CH, 1))
                pe.wait_ge(decay_rep_done, upto(b, u, 1, 0))
                for c in range(CH):
                    for t in range(KT):
                        at = (c * KT + t) * P
                        last = nc.tensor.transpose(front_b[:, at:at + P], decay_rep[:, c, t * P:t * P + P], ident_sb[:])
                last.then_inc(front_full, 1)

            def scores(b, u, c, g):
                if not exists(b):
                    return
                par = u % 2
                pe.wait_ge(k_stack_done, upto(b, u, CH, c))
                pe.wait_ge(q_diag_done, upto(b, u, 2 * CH, 2 * c + 1))
                if started(upto(b, u, 4 * CH, 4 * c + g) - 2):
                    pe.wait_ge(mask_done, upto(b, u, 4 * CH, 4 * c + g) - 2)
                for i in range(2):
                    last = mm(score_bank[g % 2][:, i * 2 * P:(i + 1) * 2 * P], k_stack[:, par, c, 2 * g + i],
                              q_diag[:, par, c, 2 * g + i].rearrange("p s n -> p (s n)"), start=True, stop=True)
                last.then_inc(score_full, 1)

            def state_update(b, u, c):
                if not exists(b):
                    return
                par = u % 2
                pe.wait_ge(v_pad_done, upto(b, u, CH, c))
                if started(upto(b, u, CH, c) - 1):
                    pe.wait_ge(attn_done, upto(b, u, CH, c) - 1)
                for t in range(KT):
                    mm(attn_bank[:, (2 + t) * P:(3 + t) * P], qk[:, par, c, D + t * P:D + t * P + P],
                       v_heads(par, c, t * H // KT, H // KT), start=(t == 0), stop=False, skip_group_check=True)

            def values(b, u, c, half):
                if not exists(b):
                    return
                par = u % 2
                pe.wait_ge(mask_done, upto(b, u, 4 * CH, 4 * c + 2 * half + 1))
                for odd in range(2):
                    for q in range(4):
                        h = 2 * q + odd
                        last = mm(attn_bank[32 * q:32 * q + 32, half * P:half * P + P], v_pad[:, par, c, 8 * half + h],
                                  masked[:, 2 * half + h // 4, (h % 4) * P:(h % 4 + 1) * P],
                                  start=False, stop=False, skip_group_check=True)
                last.then_inc(values_done, 1)

            def carried(b, u, c):
                if not exists(b):
                    return
                pe.wait_ge(q_t_done, upto(b, u, 1, 0))
                if started(upto(b, u, CH, c) - 1):
                    pe.wait_ge(state_diag_done, upto(b, u, CH, c) - 1)
                for t in range(KT):
                    last = mm(attn_bank[:, t * P:t * P + P], state_diag[:, t], q_t[:, u % 2, c, t],
                              start=False, stop=True, skip_group_check=True)
                last.then_inc(attn_full, 1)

            def hidden(b, u, q):
                if not exists(b):
                    return
                bank = hid_bank[q % 2]
                if started(upto(b, u, 4, q) - 2):
                    pe.wait_ge(relu_done, upto(b, u, 4, q) - 2)
                for i in range(2):
                    j = 2 * q + i
                    n = 0
                    for t in range(KT):
                        for lhs, rhs in ((wfc_h, xt_h), (wfc_h, xt_l), (wfc_l, xt_h)):
                            last = mm(bank[:, i * UNIT:(i + 1) * UNIT], lhs[:, t, j * P:j * P + P], rhs[:, u, :, t],
                                      start=(n == 0), stop=(n == 3 * KT - 1))
                            n += 1
                last.then_inc(hid_full, 1)

            def projected(b, u, q):
                if not exists(b):
                    return
                if q == 0:
                    pb, pu = unit_after(b, u, -1)
                    if exists(pb):
                        pe.wait_ge(y_scaled_done, upto(pb, pu, 1, 0))
                pe.wait_ge(sq_l_done, upto(b, u, 4, q))
                for i in range(2):
                    for c in range(CH):
                        for n, part in enumerate((sq_h, sq_l)):
                            at = i * UNIT + c * P
                            last = mm(y_bank[:, c * D:(c + 1) * D], part[:, q, at:at + P], wproj_t[:, 2 * q + i],
                                      start=(q == i == c == n == 0), stop=False, skip_group_check=True)
                last.then_inc(proj_done, 1)

            def attn_projected(b, u):
                if not exists(b):
                    return
                par = u % 2
                pe.wait_ge(attn_l_done, upto(b, u, CH, CH - 1))
                for c in range(CH):
                    for t in range(KT):
                        for lhs, rhs in ((attn_h, wo_h), (attn_h, wo_l), (attn_l, wo_h)):
                            last = mm(y_bank[:, c * D:(c + 1) * D], lhs[:, par, c, t], rhs[:, t],
                                      start=False, stop=True, skip_group_check=True)
                last.then_inc(y_full, 1)

            def slot(b, u):
                nxt, prev, after = unit_after(b, u, 1), unit_after(b, u, -1), unit_after(b, u, 2)
                scores(b, u, 0, 0)
                scores(b, u, 0, 1)
                project(*nxt, 0)
                scores(b, u, 0, 2)
                scores(b, u, 0, 3)
                hidden(*prev, 0)
                state_update(b, u, 0)
                values(b, u, 0, 0)
                project(*nxt, 1)
                values(b, u, 0, 1)
                carried(b, u, 0)
                hidden(*prev, 1)
                scores(b, u, 1, 0)
                scores(b, u, 1, 1)
                projected(*prev, 0)
                stack_keys(*nxt, 0)
                hidden(*prev, 2)
                scores(b, u, 1, 2)
                scores(b, u, 1, 3)
                cumulate(*nxt)
                state_update(b, u, 1)
                values(b, u, 1, 0)
                projected(*prev, 1)
                stack_queries(*nxt, 0)
                queries_t(*nxt)
                hidden(*prev, 3)
                stack_keys(*nxt, 1)
                values(b, u, 1, 1)
                carried(b, u, 1)
                projected(*prev, 2)
                stack_queries(*nxt, 1)
                projected(*prev, 3)
                decay_rows(*nxt)
                tokens_t(*after)
                attn_projected(*prev)

            setup()
            tokens_t(0, 0)
            slot(-1, NU - 1)
            for u in range(NU):
                slot(0, u)
            with pe.Fori(1, B - 1) as b:
                for u in range(NU):
                    slot(b, u)
            for u in range(NU):
                slot(B - 1, u)
            slot(B, 0)


def kernel(**inputs):
    import concourse.bacc as _bacc
    from concourse.bass_utils import run_bass_kernel_spmd as _run

    a = {k: np.asarray(v) for k, v in inputs.items()}
    heads = np.arange(D) // HD
    arrays = {
        "x": a["L0_attn_x"],
        "wq_t": a["L0_attn_Wq"].T, "wk_t": a["L0_attn_Wk"].T, "wv_t": a["L0_attn_Wv"].T, "wo_t": a["L0_attn_Wo"].T,
        "wq": a["L0_attn_Wq"], "wk": a["L0_attn_Wk"],
        "gw": np.tile(a["L0_attn_gw"].reshape(HD), H).reshape(KT, P).T,
        "sw": np.tile(a["L0_attn_sw"].reshape(HD), H).reshape(KT, P).T,
        "fb_t": a["L0_ffn_fast_b"].T, "v": a["L0_ffn_v"], "u_t": a["L0_ffn_u"].T,
        "gate": np.broadcast_to(a["L0_ffn_gate"].reshape(1, 1), (RANK, 1)),
        "w_fc": a["L0_ffn_w_fc"], "w_proj": a["L0_ffn_w_proj"],
        "ident": np.eye(P, dtype=np.float32),
        "causal": np.triu(np.ones((P, P), np.float32)),
        "same_head": (heads[:P, None] == heads[None, :P]).astype(np.float32),
        "head_of": (heads[:, None] == np.arange(H)[None, :]).astype(np.float32),
    }
    arrays = {f"in_{k}": np.ascontiguousarray(v) for k, v in arrays.items()}
    nc = _bacc.Bacc("TRN2", target_bir_lowering=False, num_devices=1)
    args = [nc.dram_tensor(k, v.shape, mybir.dt.from_np(v.dtype), kind="ExternalInput").ap() for k, v in arrays.items()]
    out = nc.dram_tensor("out_y", (B, L, D), F32, kind="ExternalOutput").ap()
    gated_attention_ternary_ffn(nc, *args, out)
    r = _run(nc, [arrays], core_ids=[0])
    return r.results[0]["out_y"]
```

```python
from contextlib import ExitStack

import numpy as np

import concourse.bass as bass
from concourse import mybir

F32 = mybir.dt.float32
F32R = mybir.dt.float32r
F16 = mybir.dt.float16
I32 = mybir.dt.int32
ALU = mybir.AluOpType
ACT = mybir.ActivationFunctionType
AX = mybir.AxisListType

P = 128
B, L, D = 8, 1024, 256
H, HD = 16, 16
HID = 1024
RANK = 16
KT = D // P
HT = HID // P
UNIT = 256
CH = UNIT // P
NU = L // UNIT
PAIRS = H // 2
VG = D + 2 * H
WTOK = 2 * D + VG
EPS = 1e-5

(XT, QK0, VG0, QK1, VG1, KS0, QS0, CUM, QT, KS1, QS1, GCT) = range(12)
FILLS = 12
FRONT_A = (XT, VG0, VG1, CUM, QS0, QS1)


def unit_after(b, u, k):
    return b + (u + k) // NU, (u + k) % NU


def exists(b):
    return not isinstance(b, int) or 0 <= b < B


def upto(b, u, per_unit, k):
    return (b * NU + u) * per_unit + k + 1


def started(value):
    return not isinstance(value, int) or value > 0


def gated_attention_ternary_ffn(nc, x, w_qk, w_qkv_t, wo_t, gates, low_rank, w_fc, w_proj, shapes, out):
    x_v = x.rearrange("b l d -> (b l) d").rearrange("(t c p) d -> t p c d", c=CH, p=P)
    out_v = out.rearrange("b l d -> (b l) d").rearrange("(t c p) d -> t p c d", c=CH, p=P)

    with ExitStack() as ctx:
        def sb(name, shape, dt=F32):
            return ctx.enter_context(nc.sbuf_tensor(name, shape, dt))

        def psum(name):
            return ctx.enter_context(nc.psum_tensor(name, [P, 512], F32))

        def sem(name):
            return ctx.enter_context(nc.semaphore(name))

        shapes_sb = sb("shapes_sb", [P, 3 * P + KT * H])
        ident_sb = shapes_sb[:, 0:P]
        causal_sb = shapes_sb[:, P:2 * P]
        same_head_sb = shapes_sb[:, 2 * P:3 * P]
        head_of_sb = shapes_sb[:, 3 * P:].rearrange("p (t h) -> p t h", t=KT)
        ident16 = sb("ident16", [P, P], F16)
        ones = sb("ones", [P, P])
        w_stage = sb("w_stage", [P, KT, WTOK])
        wtok_h = sb("wtok_h", [P, KT, WTOK], F32R)
        wtok_l = sb("wtok_l", [P, KT, WTOK], F32R)
        wo_stage = sb("wo_stage", [P, KT, D])
        wo_h = sb("wo_h", [P, KT, D], F32R)
        wo_l = sb("wo_l", [P, KT, D], F32R)
        wfc_h = sb("wfc_h", [P, KT, HID], F32R)
        wfc_l = sb("wfc_l", [P, KT, HID], F32R)
        wproj_t = sb("wproj_t", [P, HT, D], F32R)
        proj_scale = sb("proj_scale", [P, D])
        unscale = sb("unscale", [P, H])
        row_max = sb("row_max", [P, 2, KT])
        head_pow = sb("head_pow", [P, 2, KT])
        head_inv = sb("head_inv", [P, 2, KT])
        head_un = sb("head_un", [P, KT])
        gates_sb = sb("gates_sb", [P, 2, KT])
        gw_col, sw_col = gates_sb[:, 0], gates_sb[:, 1]
        sw_diag = sb("sw_diag", [P, KT, H])
        low_rank_sb = sb("low_rank_sb", [RANK, RANK + D + HID + 1])
        fbt_sb = low_rank_sb[:, 0:RANK]
        v_sb = low_rank_sb[:, RANK:RANK + D]
        ut_sb = low_rank_sb[:, RANK + D:RANK + D + HID]
        gate_sb = low_rank_sb[:, RANK + D + HID:]
        fbv = sb("fbv", [RANK, D])
        fc_scale = sb("fc_scale", [P, 3, HT])
        pj_scale = sb("pj_scale", [P, 3, KT])
        inv_proj = sb("inv_proj", [P, D])
        x_sb = sb("x_sb", [P, NU, CH, D])
        stats = sb("stats", [P, CH, 6])
        moments = sb("moments", [P, 2, CH, 2])
        neg_mean = sb("neg_mean", [P, 2, CH])
        var_eps = sb("var_eps", [P, 2, CH])
        log_var = sb("log_var", [P, 2, CH])
        guess = sb("guess", [P, 2, CH])
        newton = sb("newton", [P, 2, CH, 2])
        rstd = sb("rstd", [P, 2, CH])
        xn = sb("xn", [P, 2, CH, D])
        xt_h = sb("xt_h", [P, NU, CH, KT, P], F32R)
        xt_l = sb("xt_l", [P, NU, CH, KT, P], F32R)
        qk = sb("qk", [P, 2, CH, 2 * D])
        vg = sb("vg", [P, 2, CH, VG])
        parts = sb("parts", [P, CH, 2 * H, 4, HD], F16)
        k_stack = sb("k_stack", [P, 2, CH, PAIRS, P], F16)
        q_diag = sb("q_diag", [P, 2, CH, PAIRS, 2, P], F16)
        q_t = sb("q_t", [P, 2, CH, KT, P])
        exp_neg = sb("exp_neg", [P, CH, 2 * H])
        gate_den = sb("gate_den", [P, CH, H])
        write_den = sb("write_den", [P, CH, H])
        log_den = sb("log_den", [P, CH, H])
        before = sb("before", [P, 2, CH, H])
        log_c = sb("log_c", [P, CH, H])
        decay = sb("decay", [P, CH, H])
        write_full = sb("write_full", [P, CH, H])
        write_rec = sb("write_rec", [P, CH, H])
        write = sb("write", [P, 2, CH, H])
        decay_out = sb("decay_out", [P, CH, H])
        decay_rep = sb("decay_rep", [P, CH, D])
        decay_t = sb("decay_t", [P, 2, CH, KT, P])
        v_pad = sb("v_pad", [P, 2, CH, H, 2 * HD])
        masked = sb("masked", [P, 4, 512])
        state = sb("state", [P, KT, P])
        state_diag = sb("state_diag", [P, KT, P])
        attn = sb("attn", [P, CH, KT, P])
        attn_h = sb("attn_h", [P, 2, CH, KT, P], F32R)
        attn_l = sb("attn_l", [P, 2, CH, KT, P], F32R)
        relu_sq = sb("relu_sq", [P, 4, 512])
        relu, sq = relu_sq[:, 0:2], relu_sq[:, 2:4]
        sq_h = sb("sq_h", [P, 4, 512], F32R)
        sq_l = sb("sq_l", [P, 4, 512], F32R)
        y_both = sb("y_both", [P, 4, CH, D])
        y_scaled, y_out = y_both[:, 0:2], y_both[:, 2:4]
        fc_nat = relu_sq[:].rearrange("p g n -> p (g n)").rearrange("p (t n) -> p t n", t=HT)
        pj_nat = masked[:].rearrange("p g n -> p (g n)").rearrange("p (t n) -> p t n", t=KT)
        qk_nat = y_both[:, 0:2]
        spare_a, spare_b = (y_both[:, g:g + 2].rearrange("p g c n -> p (g c n)").bitcast(F16) for g in (0, 2))
        fc_below, fc_abs = (s.rearrange("p (t n) -> p t n", t=HT) for s in (spare_a, spare_b))
        pj_below = spare_b.rearrange("p (t n) -> p t n", t=KT)
        fc_diag = qk[:, 1].rearrange("p c n -> p (c n)").rearrange("p (t n) -> p t n", t=HT)

        front_a = psum("front_a")
        front_b = psum("front_b")
        score_bank = [psum("score_a"), psum("score_b")]
        attn_bank = psum("attn_bank")
        hid_bank = [psum("hid_a"), psum("hid_b")]
        y_bank = psum("y_bank")

        x_loaded = [sem(f"x_loaded{i}") for i in range(NU)]
        heads_loaded = sem("heads_loaded")
        tokens_w_loaded = sem("tokens_w_loaded")
        fc_loaded = sem("fc_loaded")
        proj_loaded = sem("proj_loaded")
        wo_loaded = sem("wo_loaded")
        zeroed = sem("zeroed")
        setup_v = sem("setup_v")
        setup_pe = sem("setup_pe")
        abs_sums_done = sem("abs_sums_done")
        fc_diag_done = sem("fc_diag_done")
        below_done = sem("below_done")
        wtok_h_done = sem("wtok_h_done")
        ffn_fill = sem("ffn_fill")
        ffn_h_done = sem("ffn_h_done")
        stats_done = sem("stats_done")
        moments_done = sem("moments_done")
        ln_ready = sem("ln_ready")
        log_var_done = sem("log_var_done")
        guess_done = sem("guess_done")
        newton_step = sem("newton_step")
        rstd_done = sem("rstd_done")
        xn_done = sem("xn_done")
        front_full = sem("front_full")
        xt_h_done = sem("xt_h_done")
        xt_l_done = sem("xt_l_done")
        qk_done = sem("qk_done")
        vg_done = sem("vg_done")
        part_h_done = sem("part_h_done")
        part_l_done = sem("part_l_done")
        parts_done = sem("parts_done")
        k_stack_done = sem("k_stack_done")
        q_diag_done = sem("q_diag_done")
        q_t_done = sem("q_t_done")
        exp_neg_done = sem("exp_neg_done")
        dens_done = sem("dens_done")
        log_den_done = sem("log_den_done")
        before_step = sem("before_step")
        log_c_done = sem("log_c_done")
        decay_done = sem("decay_done")
        write_step = sem("write_step")
        write_done = sem("write_done")
        decay_out_done = sem("decay_out_done")
        decay_rep_done = sem("decay_rep_done")
        decay_t_done = sem("decay_t_done")
        v_pad_done = sem("v_pad_done")
        score_full = sem("score_full")
        mask_done = sem("mask_done")
        values_done = sem("values_done")
        attn_full = sem("attn_full")
        attn_done = sem("attn_done")
        state_done = sem("state_done")
        state_diag_done = sem("state_diag_done")
        attn_h_done = sem("attn_h_done")
        attn_l_done = sem("attn_l_done")
        hid_full = sem("hid_full")
        relu_done = sem("relu_done")
        sq_done = sem("sq_done")
        sq_h_done = sem("sq_h_done")
        sq_l_done = sem("sq_l_done")
        proj_done = sem("proj_done")
        y_full = sem("y_full")
        y_scaled_done = sem("y_scaled_done")
        y_out_done = sem("y_out_done")
        stored = [sem("stored_even"), sem("stored_odd")]

        V_ROW_MAX, V_HEAD_SCALES, V_SW_DIAG, V_W_STAGE, V_SMALL_READ, V_FC_SCALES, V_PJ_SCALES, V_WTOK, V_FC_TERNARY = (
            1, 5, 6, 7, 10, 12, 14, 16, 17)
        V_PJ_TERNARY, V_FC_LOW, V_DONE = 18, 22, 27
        PE_HEAD_SUM, PE_SMALL = 1, 2
        fc_banks = [hid_bank[0], hid_bank[1], y_bank, attn_bank]
        proj_banks = [*score_bank, *hid_bank]

        def heads_bc(ap, n):
            return ap.unsqueeze(len(ap.shape)).to_broadcast([*ap.shape, n])

        def v_heads(par, c, first, count):
            flat = v_pad[:, par, c].rearrange("p h x -> p (h x)")[:, first * 2 * HD:(first + count) * 2 * HD]
            return flat.rearrange("p (g s e) -> p g s e", s=4, e=HD)[:, :, 0:4:3, :]

        block = ctx.enter_context(nc.Block())

        @block.sync
        def _(sp):
            def load(b, u):
                if not exists(b):
                    return
                if started(upto(b, u, 1, 0) - NU):
                    sp.wait_ge(y_out_done, upto(b, u, 1, 0) - NU)
                sp.dma_start(x_sb[:, u], x_v[b * NU + u]).then_inc(x_loaded[u], 16)

            def store(b, u):
                if not exists(b):
                    return
                sp.wait_ge(y_out_done, upto(b, u, 1, 0))
                sp.dma_start(out_v[b * NU + u], y_out[:, u % 2]).then_inc(stored[u % 2], 16)

            def slot(b, u):
                load(*unit_after(b, u, 3))
                store(*unit_after(b, u, -1))

            load(0, 0)
            sp.dma_start(shapes_sb[:], shapes).then_inc(heads_loaded, 16)
            sp.dma_start(gates_sb[:], gates.rearrange("g p t -> p g t")).then_inc(heads_loaded, 16)
            sp.dma_start(qk_nat, w_qk.rearrange("w (t p) n -> p w t n", p=P)).then_inc(heads_loaded, 16)
            sp.dma_start(w_stage[:, :, 0:3 * D], w_qkv_t.rearrange("(t p) n -> p t n", p=P)).then_inc(tokens_w_loaded, 16)
            sp.dma_start(low_rank_sb[:], low_rank).then_inc(tokens_w_loaded, 16)
            sp.dma_start(wo_stage[:], wo_t.rearrange("(t p) n -> p t n", p=P)).then_inc(wo_loaded, 16)
            load(0, 1)
            load(0, 2)
            for u in range(NU):
                slot(0, u)
            with sp.Fori(1, B - 1) as b:
                for u in range(NU):
                    slot(b, u)
            for u in range(NU):
                slot(B - 1, u)
            slot(B, 0)
            for par in range(2):
                sp.wait_ge(stored[par], 16 * B * NU // 2)

        @block.gpsimd
        def _(pool):
            def waits_to_normalise(b, u):
                if not exists(b):
                    return
                pool.wait_ge(rstd_done, upto(b, u, 1, 0))
                if started(upto(b, u, FILLS, XT) - 2 * FILLS):
                    pool.wait_ge(front_full, upto(b, u, FILLS, XT) - 2 * FILLS)

            def normalise(b, u):
                if not exists(b):
                    return
                for c in range(CH):
                    nc.gpsimd.tensor_scalar(xn[:, u % 2, c], x_sb[:, u, c], neg_mean[:, u % 2, c:c + 1],
                                            rstd[:, u % 2, c:c + 1], ALU.add, ALU.mult).then_inc(xn_done, 1)

            def values_and_decay(b, u):
                if not exists(b):
                    return
                par = u % 2
                pool.wait_ge(write_done, upto(b, u, 1, 0))
                pool.wait_ge(vg_done, upto(b, u, CH, CH - 1))
                pb, pu = unit_after(b, u, -2)
                if exists(pb):
                    pool.wait_ge(attn_full, upto(pb, pu, CH, CH - 1))
                for c in range(CH):
                    if c == CH - 1:
                        pool.wait_ge(decay_out_done, upto(b, u, 1, 0))
                        if started(upto(b, u, FILLS, GCT) - FILLS):
                            pool.wait_ge(front_full, upto(b, u, FILLS, GCT) - FILLS)
                    val = vg[:, par, c, 0:D].rearrange("p (g s e) -> p g s e", s=2, e=HD)
                    fac = heads_bc(write[:, par, c], HD).rearrange("p (g s) e -> p g s e", s=2)
                    nc.gpsimd.tensor_tensor(v_heads(par, c, 0, H), val, fac, ALU.mult).then_inc(v_pad_done, 1)
                nc.gpsimd.tensor_scalar(decay_rep[:].rearrange("p c (h e) -> p (c h) e", e=HD),
                                        heads_bc(decay_out[:].rearrange("p c h -> p (c h)"), HD), 1.0, 1.0,
                                        ALU.mult, ALU.mult).then_inc(decay_rep_done, 1)

            def diagonal_state(b, u, c):
                if not exists(b):
                    return
                pool.wait_ge(state_done, upto(b, u, CH, c))
                if (u, c) != (NU - 1, CH - 1):
                    nc.gpsimd.tensor_tensor(state_diag[:], state[:],
                                            same_head_sb.unsqueeze(1).to_broadcast([P, KT, P]),
                                            ALU.mult).then_inc(state_diag_done, 1)

            def attn_parts(b, u, c):
                if not exists(b):
                    return
                pb, pu = unit_after(b, u, -2)
                if exists(pb):
                    pool.wait_ge(y_full, upto(pb, pu, 1, 0))
                pool.wait_ge(attn_done, upto(b, u, CH, c))
                nc.gpsimd.tensor_tensor(attn_h[:, u % 2, c], attn[:, c], ones[:].unsqueeze(1).to_broadcast([P, KT, P]),
                                        ALU.mult).then_inc(attn_h_done, 1)
                pool.wait_ge(attn_h_done, upto(b, u, CH, c))
                nc.gpsimd.tensor_tensor(attn_l[:, u % 2, c], attn[:, c], attn_h[:, u % 2, c].bitcast(F32),
                                        ALU.subtract).then_inc(attn_l_done, 1)
                if (u, c) == (NU - 1, CH - 1):
                    nc.gpsimd.memset(state_diag[:], 0.0).then_inc(state_diag_done, 1)

            def residual(b, u):
                if not exists(b):
                    return
                pool.wait_ge(y_scaled_done, upto(b, u, 1, 0))
                pb, pu = unit_after(b, u, -2)
                if exists(pb):
                    pool.wait_ge(stored[u % 2], (pb * (NU // 2) + pu // 2 + 1) * 16)
                nc.gpsimd.tensor_tensor(y_out[:, u % 2], y_scaled[:, u % 2], x_sb[:, u], ALU.add).then_inc(y_out_done, 1)

            def slot(b, u):
                nxt, prev, after = unit_after(b, u, 1), unit_after(b, u, -1), unit_after(b, u, 2)
                diagonal_state(b, u, 0)
                attn_parts(b, u, 0)
                waits_to_normalise(*after)
                values_and_decay(*nxt)
                normalise(*after)
                diagonal_state(b, u, 1)
                attn_parts(b, u, 1)
                residual(*prev)

            def below(nat, tiles, scales, low):
                for t in range(tiles):
                    last = nc.gpsimd.tensor_scalar(low[:, t], nat[:, t], scales[:, 2, t:t + 1], None, ALU.is_lt)
                last.then_inc(below_done, 1)

            nc.gpsimd.memset(state_diag[:], 0.0).then_inc(zeroed, 1)
            nc.gpsimd.memset(ones[:], 1.0).then_inc(zeroed, 1)
            waits_to_normalise(0, 0)
            normalise(0, 0)
            nc.gpsimd.memset(v_pad[:], 0.0).then_inc(zeroed, 1)
            nc.gpsimd.memset(q_diag[:], 0.0).then_inc(zeroed, 1)
            pool.wait_ge(setup_v, V_FC_SCALES)
            below(fc_nat, HT, fc_scale, fc_below)
            pool.wait_ge(setup_v, V_PJ_SCALES)
            below(pj_nat, KT, pj_scale, pj_below)
            pool.wait_ge(zeroed, 4)
            slot(-1, NU - 1)
            for u in range(NU):
                slot(0, u)
            with pool.Fori(1, B - 1) as b:
                for u in range(NU):
                    slot(b, u)
            for u in range(NU):
                slot(B - 1, u)
            slot(B, 0)

        @block.scalar
        def _(act):
            def filled(b, u, fill):
                act.wait_ge(front_full, upto(b, u, FILLS, fill))
                return front_a if fill in FRONT_A else front_b

            def rstd_guess(b, u):
                if not exists(b):
                    return
                par = u % 2
                act.wait_ge(ln_ready, upto(b, u, 1, 0))
                nc.scalar.activation(log_var[:, par], var_eps[:, par], ACT.Ln).then_inc(log_var_done, 1)
                act.wait_ge(log_var_done, upto(b, u, 1, 0))
                nc.scalar.activation(guess[:, par], log_var[:, par], ACT.Exp, scale=-0.5).then_inc(guess_done, 1)

            def xt_high(b, u):
                if not exists(b):
                    return
                bank = filled(b, u, XT)
                pb, pu = unit_after(b, u, -NU)
                if exists(pb):
                    act.wait_ge(hid_full, upto(pb, pu, 4, 3))
                nc.scalar.activation(xt_h[:, u], bank[:].rearrange("p (c t n) -> p c t n", c=CH, t=KT),
                                     ACT.Copy).then_inc(xt_h_done, 1)

            def projected(b, u, c):
                if not exists(b):
                    return
                par = u % 2
                bank = filled(b, u, [QK0, QK1][c])
                pb, pu = unit_after(b, u, -2)
                if exists(pb):
                    act.wait_ge(attn_full, upto(pb, pu, CH, CH - 1))
                    act.wait_ge(v_pad_done, upto(pb, pu, CH, CH - 1))
                nc.scalar.activation(qk[:, par, c], bank[:], ACT.Copy).then_inc(qk_done, 1)
                pb, pu = unit_after(b, u, -1)
                if exists(pb):
                    act.wait_ge(front_full, upto(pb, pu, FILLS, QS1))
                nc.scalar.activation(parts[:, c, :, 0, :], bank[:].rearrange("p (h e) -> p h e", e=HD),
                                     ACT.Copy).then_inc(part_h_done, 1)
                bank = filled(b, u, [VG0, VG1][c])
                nc.scalar.activation(vg[:, par, c], bank[:, 0:VG], ACT.Copy).then_inc(vg_done, 1)

            def gate_exp(b, u):
                if not exists(b):
                    return
                act.wait_ge(vg_done, upto(b, u, CH, CH - 1))
                pb, pu = unit_after(b, u, -1)
                if exists(pb):
                    act.wait_ge(dens_done, upto(pb, pu, 2, 1))
                nc.scalar.activation(exp_neg[:], vg[:, u % 2, :, D:VG], ACT.Exp, scale=-1.0).then_inc(exp_neg_done, 1)

            def gate_log(b, u):
                if not exists(b):
                    return
                act.wait_ge(dens_done, upto(b, u, 2, 1))
                pb, pu = unit_after(b, u, -1)
                if exists(pb):
                    act.wait_ge(front_full, upto(pb, pu, FILLS, CUM))
                    act.wait_ge(before_step, upto(pb, pu, 2, 1))
                nc.scalar.activation(log_den[:], gate_den[:], ACT.Ln).then_inc(log_den_done, 1)

            def keys_stacked(b, u, c):
                if not exists(b):
                    return
                bank = filled(b, u, [KS0, KS1][c])
                pb, pu = unit_after(b, u, -2)
                if exists(pb):
                    act.wait_ge(score_full, upto(pb, pu, 4 * CH, 4 * CH - 1))
                nc.scalar.activation(k_stack[:, u % 2, c], bank[:].bitcast(F16).rearrange("p (g n) -> p g n", g=PAIRS),
                                     ACT.Copy).then_inc(k_stack_done, 1)

            def queries_stacked(b, u, c):
                if not exists(b):
                    return
                bank = filled(b, u, [QS0, QS1][c])
                if isinstance(b, int) and b == 0 and u < 2:
                    act.wait_ge(zeroed, 4)
                for half in range(2):
                    rows = slice(64 * half, 64 * half + 64)
                    nc.scalar.activation(q_diag[rows, u % 2, c, :, half, :],
                                         bank[rows].bitcast(F16).rearrange("p (g n) -> p g n", g=PAIRS),
                                         ACT.Copy).then_inc(q_diag_done, 1)

            def query_t(b, u):
                if not exists(b):
                    return
                bank = filled(b, u, QT)
                nc.scalar.activation(q_t[:, u % 2], bank[:].rearrange("p (c t n) -> p c t n", c=CH, t=KT),
                                     ACT.Copy).then_inc(q_t_done, 1)

            def decay_exp(b, u):
                if not exists(b):
                    return
                act.wait_ge(log_c_done, upto(b, u, 1, 0))
                pb, pu = unit_after(b, u, -1)
                if exists(pb):
                    act.wait_ge(decay_out_done, upto(pb, pu, 1, 0))
                nc.scalar.activation(decay[:], log_c[:], ACT.Exp, scale=-1.0).then_inc(decay_done, 1)

            def decay_transposed(b, u):
                if not exists(b):
                    return
                bank = filled(b, u, GCT)
                pb, pu = unit_after(b, u, -2)
                if exists(pb):
                    act.wait_ge(attn_done, upto(pb, pu, CH, CH - 1))
                nc.scalar.activation(decay_t[:, u % 2], bank[:].rearrange("p (c t n) -> p c t n", c=CH, t=KT),
                                     ACT.Copy).then_inc(decay_t_done, 1)

            def squares(b, u, q):
                if not exists(b):
                    return
                n = q % 2
                act.wait_ge(hid_full, upto(b, u, 4, q))
                nc.scalar.activation(relu[:, n], hid_bank[n][:], ACT.Relu).then_inc(relu_done, 1)
                if started(upto(b, u, 4, q) - 2):
                    act.wait_ge(sq_l_done, upto(b, u, 4, q) - 2)
                act.wait_ge(relu_done, upto(b, u, 4, q))
                nc.scalar.activation(sq[:, n], relu[:, n], ACT.Square).then_inc(sq_done, 1)

            def slot(b, u):
                nxt, prev, after = unit_after(b, u, 1), unit_after(b, u, -1), unit_after(b, u, 2)
                projected(*nxt, 0)
                squares(*prev, 0)
                projected(*nxt, 1)
                gate_exp(*nxt)
                keys_stacked(*nxt, 0)
                gate_log(*nxt)
                queries_stacked(*nxt, 0)
                squares(*prev, 1)
                squares(*prev, 2)
                rstd_guess(*after)
                decay_exp(*nxt)
                query_t(*nxt)
                squares(*prev, 3)
                keys_stacked(*nxt, 1)
                queries_stacked(*nxt, 1)
                decay_transposed(*nxt)
                xt_high(*after)

            def abs_sums(nat, tiles, scales, scratch):
                for t in range(tiles):
                    last = nc.scalar.activation(scratch[:, t], nat[:, t], ACT.Abs, accum_out=scales[:, 0, t:t + 1])
                last.then_inc(abs_sums_done, 1)

            def fc_diagonals():
                act.wait_ge(heads_loaded, 16 * 3)
                act.wait_ge(setup_v, V_FC_SCALES)
                for t in range(HT):
                    last = nc.scalar.activation(fc_diag[:, t], ident_sb, ACT.Copy, scale=fc_scale[:, 0, t:t + 1])
                last.then_inc(fc_diag_done, 1)

            def token_weights_high():
                act.wait_ge(setup_v, V_W_STAGE)
                nc.scalar.activation(wtok_h[:], w_stage[:], ACT.Copy).then_inc(wtok_h_done, 1)

            def fc_high(i):
                act.wait_ge(ffn_fill, i + 1)
                nc.scalar.activation(wfc_h[:, i // 2, 512 * (i % 2):512 * (i % 2) + 512], fc_banks[i][:],
                                     ACT.Copy).then_inc(ffn_h_done, 1)

            def proj_taken(i):
                act.wait_ge(ffn_fill, 4 + i + 1)
                nc.scalar.activation(wproj_t[:, 2 * i:2 * i + 2, :], proj_banks[i][:].rearrange("p (t n) -> p t n", t=2),
                                     ACT.Copy).then_inc(ffn_h_done, 1)

            def set_up():
                first, second = (0, 0), (0, 1)
                rstd_guess(*first)
                act.wait_ge(fc_loaded, 16)
                abs_sums(fc_nat, HT, fc_scale, fc_abs)
                act.wait_ge(proj_loaded, 16)
                act.wait_ge(abs_sums_done, 1)
                abs_sums(pj_nat, KT, pj_scale, pj_below)
                xt_high(*first)
                token_weights_high()
                fc_diagonals()
                projected(*first, 0)
                projected(*first, 1)
                gate_exp(*first)
                gate_log(*first)
                fc_high(0)
                fc_high(1)
                keys_stacked(*first, 0)
                queries_stacked(*first, 0)
                fc_high(2)
                fc_high(3)
                rstd_guess(*second)
                decay_exp(*first)
                proj_taken(0)
                query_t(*first)
                proj_taken(1)
                keys_stacked(*first, 1)
                queries_stacked(*first, 1)
                proj_taken(2)
                proj_taken(3)
                decay_transposed(*first)
                xt_high(*second)

            nc.scalar.preload_act_table_set("natural_log_exp_and_others")
            act.dma_start(fc_nat, w_fc.rearrange("(t p) n -> p t n", p=P)).then_inc(fc_loaded, 16)
            act.dma_start(pj_nat, w_proj.rearrange("(t p) n -> p t n", p=P)).then_inc(proj_loaded, 16)
            set_up()
            for u in range(NU):
                slot(0, u)
            with act.Fori(1, B - 1) as b:
                for u in range(NU):
                    slot(b, u)
            for u in range(NU):
                slot(B - 1, u)
            slot(B, 0)

        @block.vector
        def _(dve):
            steps = [0]

            def count(ins):
                steps[0] += 1
                ins.then_inc(setup_v, 1)

            def step(ins):
                count(ins)
                dve.wait_ge(setup_v, steps[0])

            def head_scales():
                step(nc.vector.tensor_reduce(row_max[:].rearrange("p w t -> p (w t)"),
                                             qk_nat.rearrange("p w t n -> p (w t) n"), AX.X, ALU.max,
                                             apply_absolute_value=True))
                assert steps[0] == V_ROW_MAX
                dve.wait_ge(setup_pe, PE_HEAD_SUM)
                pow2 = head_pow[:].rearrange("p w t -> p (w t)")
                step(nc.vector.tensor_scalar(pow2, score_bank[0][:, 0:2 * KT], 1e-30, None, ALU.max))
                step(nc.vector.tensor_scalar(pow2.bitcast(I32), pow2.bitcast(I32), 0x7F800000, None, ALU.bitwise_and))
                step(nc.vector.reciprocal(head_inv[:].rearrange("p w t -> p (w t)"), pow2))
                count(nc.vector.tensor_tensor(head_un[:], head_pow[:, 0], head_pow[:, 1], ALU.mult))
                assert steps[0] == V_HEAD_SCALES
                nc.vector.tensor_scalar(sw_diag[:, 0], head_of_sb[:, 0], sw_col[:, 0:1], None, ALU.mult)
                count(nc.vector.tensor_scalar(sw_diag[:, 1], head_of_sb[:, 1], sw_col[:, 1:2], None, ALU.mult))
                assert steps[0] == V_SW_DIAG

            def token_weights():
                for t in range(KT):
                    nc.vector.tensor_scalar(w_stage[:, t, 3 * D:3 * D + H], head_of_sb[:, t], gw_col[:, t:t + 1], None,
                                            ALU.mult)
                dve.wait_ge(setup_pe, PE_SMALL)
                nc.vector.tensor_copy(w_stage[:, :, 3 * D + H:WTOK],
                                      hid_bank[1][:, 0:KT * H].rearrange("p (t h) -> p t h", t=KT))
                dve.wait_ge(tokens_w_loaded, 16 * 2)
                cols = w_stage[:, :, 0:2 * D]
                count(nc.vector.tensor_tensor(cols, cols, hid_bank[0][:].unsqueeze(1).to_broadcast([P, KT, 2 * D]),
                                              ALU.mult))
                assert steps[0] == V_W_STAGE
                count(nc.vector.tensor_scalar(unscale[:], score_bank[1][:, 0:H], 1.0 / HD, None, ALU.mult))
                count(nc.vector.tensor_copy(fbv[:], score_bank[0][0:RANK, 0:D]))
                count(nc.vector.tensor_scalar(ut_sb, ut_sb, gate_sb[:, 0:1], None, ALU.mult))
                assert steps[0] == V_SMALL_READ

            def scales_of(scales, width):
                step(nc.vector.tensor_scalar(scales[:, 0], scales[:, 0], 1.0 / width, 1e-5, ALU.mult, ALU.max))
                nc.vector.tensor_scalar(scales[:, 1], scales[:, 0], 0.5, None, ALU.mult)
                count(nc.vector.tensor_scalar(scales[:, 2], scales[:, 0], -0.5, None, ALU.mult))

            def ternary(nat, tiles, scales, low):
                for t in range(tiles):
                    last = nc.vector.scalar_tensor_tensor(out=nat[:, t], in0=nat[:, t], scalar=scales[:, 1, t:t + 1],
                                                          in1=low[:, t], op0=ALU.is_gt, op1=ALU.subtract)
                count(last)

            def fc_low(i):
                cols = wfc_h[:, i // 2, 512 * (i % 2):512 * (i % 2) + 512]
                dve.wait_ge(ffn_h_done, i + 1)
                count(nc.vector.tensor_tensor(wfc_l[:, i // 2, 512 * (i % 2):512 * (i % 2) + 512], fc_banks[i][:],
                                              cols.bitcast(F32), ALU.subtract))

            def output_weights():
                dve.wait_ge(ffn_fill, 9)
                step(nc.vector.tensor_copy(proj_scale[:], y_bank[:, 0:D]))
                step(nc.vector.reciprocal(inv_proj[:], proj_scale[:]))
                dve.wait_ge(wo_loaded, 16)
                step(nc.vector.tensor_tensor(wo_stage[:], wo_stage[:], inv_proj[:].unsqueeze(1).to_broadcast([P, KT, D]),
                                             ALU.mult))
                step(nc.vector.tensor_copy(wo_h[:], wo_stage[:]))
                count(nc.vector.tensor_tensor(wo_l[:], wo_stage[:], wo_h[:].bitcast(F32), ALU.subtract))
                assert steps[0] == V_DONE

            def set_up():
                first, second = (0, 0), (0, 1)
                nc.vector.memset(before[:], 0.0)
                stats_of(*first)
                waits_for_stats(*first)
                moments_of(*first)
                scalars_of(*first)
                refine_rstd(*first)
                dve.wait_ge(heads_loaded, 16 * 3)
                nc.vector.tensor_copy(ident16[:], ident_sb)
                head_scales()
                token_weights()
                dve.wait_ge(abs_sums_done, 1)
                scales_of(fc_scale, D)
                assert steps[0] == V_FC_SCALES
                dve.wait_ge(abs_sums_done, 2)
                scales_of(pj_scale, HID)
                assert steps[0] == V_PJ_SCALES
                xt_low(*first)
                dve.wait_ge(wtok_h_done, 1)
                for t in range(KT):
                    count(nc.vector.tensor_tensor(wtok_l[:, t], w_stage[:, t], wtok_h[:, t].bitcast(F32), ALU.subtract))
                assert steps[0] == V_WTOK
                dve.wait_ge(below_done, 1)
                ternary(fc_nat, HT, fc_scale, fc_below)
                assert steps[0] == V_FC_TERNARY
                qk_parts(*first, 0)
                dve.wait_ge(below_done, 2)
                ternary(pj_nat, KT, pj_scale, pj_below)
                assert steps[0] == V_PJ_TERNARY
                dens(*first)
                qk_parts(*first, 1)
                sums_before(*first)
                stats_of(*second)
                waits_for_stats(*second)
                moments_of(*second)
                scalars_of(*second)
                fc_low(0)
                fc_low(1)
                fc_low(2)
                fc_low(3)
                clip_log(*first)
                assert steps[0] == V_FC_LOW
                refine_rstd(*second)
                decays(*first)
                output_weights()
                xt_low(*second)

            def stats_of(b, u):
                if not exists(b):
                    return
                dve.wait_ge(x_loaded[u], (b + 1) * 16)
                for c in range(CH):
                    last = nc.vector.bn_stats(stats[:, c], x_sb[:, u, c])
                last.then_inc(stats_done, 1)

            def waits_for_stats(b, u):
                if not exists(b):
                    return
                dve.wait_ge(stats_done, upto(b, u, 1, 0))

            def moments_of(b, u):
                if not exists(b):
                    return
                for c in range(CH):
                    last = nc.vector.bn_aggr(moments[:, u % 2, c], stats[:, c])
                last.then_inc(moments_done, 1)

            def scalars_of(b, u):
                if not exists(b):
                    return
                par = u % 2
                pb, pu = unit_after(b, u, -2)
                if exists(pb):
                    dve.wait_ge(xn_done, upto(pb, pu, CH, CH - 1))
                dve.wait_ge(moments_done, upto(b, u, 1, 0))
                nc.vector.tensor_scalar(neg_mean[:, par], moments[:, par, :, 0], -1.0, None, ALU.mult)
                nc.vector.tensor_scalar(var_eps[:, par], moments[:, par, :, 1], EPS, None, ALU.add).then_inc(ln_ready, 1)

            def refine_rstd(b, u):
                if not exists(b):
                    return
                par = u % 2
                y, a = guess[:, par], var_eps[:, par]
                sqr, corr = newton[:, par, :, 0], newton[:, par, :, 1]
                dve.wait_ge(guess_done, upto(b, u, 1, 0))
                dve.wait_ge(ln_ready, upto(b, u, 1, 0))
                nc.vector.tensor_tensor(sqr, y, y, ALU.mult).then_inc(newton_step, 1)
                dve.wait_ge(newton_step, upto(b, u, 2, 0))
                nc.vector.scalar_tensor_tensor(out=corr, in0=sqr, scalar=-0.5, in1=a, op0=ALU.mult,
                                               op1=ALU.mult).then_inc(newton_step, 1)
                dve.wait_ge(newton_step, upto(b, u, 2, 1))
                nc.vector.scalar_tensor_tensor(out=rstd[:, par], in0=corr, scalar=1.5, in1=y, op0=ALU.add,
                                               op1=ALU.mult).then_inc(rstd_done, 1)

            def xt_low(b, u):
                if not exists(b):
                    return
                dve.wait_ge(xt_h_done, upto(b, u, 1, 0))
                nc.vector.tensor_tensor(xt_l[:, u], front_a[:].rearrange("p (c t n) -> p c t n", c=CH, t=KT),
                                        xt_h[:, u].bitcast(F32), ALU.subtract).then_inc(xt_l_done, 1)

            def qk_parts(b, u, c):
                if not exists(b):
                    return
                src = qk[:, u % 2, c].rearrange("p (h e) -> p h e", e=HD)
                dve.wait_ge(part_h_done, upto(b, u, CH, c))
                nc.vector.tensor_tensor(parts[:, c, :, 2, :], src, parts[:, c, :, 0, :],
                                        ALU.subtract).then_inc(part_l_done, 1)
                dve.wait_ge(part_l_done, upto(b, u, CH, c))
                q, k = parts[:, c, 0:H], parts[:, c, H:2 * H]
                nc.vector.tensor_copy(q[:, :, 1::2, :], q[:, :, 0::2, :])
                nc.vector.tensor_copy(k[:, :, 3, :], k[:, :, 0, :])
                nc.vector.tensor_copy(k[:, :, 1, :], k[:, :, 2, :]).then_inc(parts_done, 1)

            def dens(b, u):
                if not exists(b):
                    return
                dve.wait_ge(exp_neg_done, upto(b, u, 1, 0))
                pb, pu = unit_after(b, u, -1)
                if exists(pb):
                    dve.wait_ge(log_den_done, upto(pb, pu, 1, 0))
                nc.vector.tensor_scalar(gate_den[:], exp_neg[:, :, 0:H], 1.0, 1e6, ALU.add, ALU.min).then_inc(dens_done, 1)
                nc.vector.tensor_scalar(write_den[:], exp_neg[:, :, H:2 * H], 1.0, None, ALU.add).then_inc(dens_done, 1)

            def sums_before(b, u):
                if not exists(b):
                    return
                par = u % 2
                dve.wait_ge(log_den_done, upto(b, u, 1, 0))
                if started(upto(b, u, 2, 0) - 1):
                    dve.wait_ge(before_step, upto(b, u, 2, 0) - 1)
                nc.vector.tensor_tensor(before[:, par, 1], before[:, par, 0], log_den[:, 0], ALU.add).then_inc(before_step, 1)
                dve.wait_ge(before_step, upto(b, u, 2, 0))
                if u == NU - 1:
                    nc.vector.memset(before[:, 1 - par, 0], 0.0).then_inc(before_step, 1)
                else:
                    nc.vector.tensor_tensor(before[:, 1 - par, 0], before[:, par, 1], log_den[:, 1],
                                            ALU.add).then_inc(before_step, 1)

            def clip_log(b, u):
                if not exists(b):
                    return
                dve.wait_ge(front_full, upto(b, u, FILLS, CUM))
                pb, pu = unit_after(b, u, -1)
                if exists(pb):
                    dve.wait_ge(decay_done, upto(pb, pu, 1, 0))
                nc.vector.tensor_scalar(log_c[:], front_a[:, 0:CH * H].rearrange("p (c h) -> p c h", c=CH), 30.0, -30.0,
                                        ALU.min, ALU.max).then_inc(log_c_done, 1)

            def decays(b, u):
                if not exists(b):
                    return
                par = u % 2
                dve.wait_ge(decay_done, upto(b, u, 1, 0))
                nc.vector.scalar_tensor_tensor(out=write_full[:], in0=decay[:], scalar=1e-6, in1=write_den[:],
                                               op0=ALU.add, op1=ALU.mult).then_inc(write_step, 1)
                dve.wait_ge(write_step, upto(b, u, 2, 0))
                nc.vector.reciprocal(write_rec[:], write_full[:]).then_inc(write_step, 1)
                pb, pu = unit_after(b, u, -2)
                if exists(pb):
                    dve.wait_ge(v_pad_done, upto(pb, pu, CH, CH - 1))
                dve.wait_ge(write_step, upto(b, u, 2, 1))
                nc.vector.tensor_tensor(write[:, par], write_rec[:], vg[:, par, :, D + H:VG], ALU.mult).then_inc(write_done, 1)
                pb, pu = unit_after(b, u, -1)
                if exists(pb):
                    dve.wait_ge(decay_rep_done, upto(pb, pu, 1, 0))
                nc.vector.scalar_tensor_tensor(out=decay_out[:], in0=decay[:], scalar=1e-6,
                                               in1=unscale[:].unsqueeze(1).to_broadcast([P, CH, H]),
                                               op0=ALU.add, op1=ALU.mult).then_inc(decay_out_done, 1)

            def mask(b, u, c, g):
                if not exists(b):
                    return
                dve.wait_ge(score_full, upto(b, u, 4 * CH, 4 * c + g))
                if started(upto(b, u, 2 * CH, 2 * c + g // 2) - 2):
                    dve.wait_ge(values_done, upto(b, u, 2 * CH, 2 * c + g // 2) - 2)
                nc.vector.tensor_tensor(masked[:, g].rearrange("p (h n) -> p h n", h=4),
                                        score_bank[g % 2][:].rearrange("p (h n) -> p h n", h=4),
                                        causal_sb.unsqueeze(1).to_broadcast([P, 4, P]), ALU.mult).then_inc(mask_done, 1)

            def chunk_out(b, u, c):
                if not exists(b):
                    return
                par = u % 2
                dve.wait_ge(attn_full, upto(b, u, CH, c))
                update = attn_bank[:, 2 * P:4 * P].rearrange("p (t n) -> p t n", t=KT)
                if started(upto(b, u, CH, c) - 1):
                    dve.wait_ge(state_diag_done, upto(b, u, CH, c) - 1)
                if (u, c) == (0, 0):
                    nc.vector.tensor_copy(state[:], update).then_inc(state_done, 1)
                else:
                    if started(upto(b, u, CH, c) - 1):
                        dve.wait_ge(state_done, upto(b, u, CH, c) - 1)
                    nc.vector.tensor_tensor(state[:], state[:], update, ALU.add).then_inc(state_done, 1)
                dve.wait_ge(decay_t_done, upto(b, u, 1, 0))
                pb, pu = unit_after(b, u, -1)
                if exists(pb):
                    dve.wait_ge(attn_l_done, upto(pb, pu, CH, c))
                nc.vector.tensor_tensor(attn[:, c], attn_bank[:, 0:2 * P].rearrange("p (t n) -> p t n", t=KT),
                                        decay_t[:, par, c], ALU.mult).then_inc(attn_done, 1)

            def split_squares(b, u, q):
                if not exists(b):
                    return
                n = q % 2
                dve.wait_ge(sq_done, upto(b, u, 4, q))
                if started(upto(b, u, 4, q) - 4):
                    dve.wait_ge(proj_done, upto(b, u, 4, q) - 4)
                nc.vector.tensor_copy(sq_h[:, q], sq[:, n]).then_inc(sq_h_done, 1)
                dve.wait_ge(sq_h_done, upto(b, u, 4, q))
                nc.vector.tensor_tensor(sq_l[:, q], sq[:, n], sq_h[:, q].bitcast(F32), ALU.subtract).then_inc(sq_l_done, 1)

            def scale_y(b, u):
                if not exists(b):
                    return
                dve.wait_ge(y_full, upto(b, u, 1, 0))
                pb, pu = unit_after(b, u, -2)
                if exists(pb):
                    dve.wait_ge(y_out_done, upto(pb, pu, 1, 0))
                nc.vector.tensor_tensor(y_scaled[:, u % 2], y_bank[:].rearrange("p (c n) -> p c n", c=CH),
                                        proj_scale[:].unsqueeze(1).to_broadcast([P, CH, D]),
                                        ALU.mult).then_inc(y_scaled_done, 1)

            def slot(b, u):
                nxt, prev, after = unit_after(b, u, 1), unit_after(b, u, -1), unit_after(b, u, 2)
                mask(b, u, 0, 0)
                mask(b, u, 0, 1)
                mask(b, u, 0, 2)
                mask(b, u, 0, 3)
                qk_parts(*nxt, 0)
                stats_of(*after)
                split_squares(*prev, 0)
                qk_parts(*nxt, 1)
                dens(*nxt)
                chunk_out(b, u, 0)
                waits_for_stats(*after)
                mask(b, u, 1, 0)
                moments_of(*after)
                mask(b, u, 1, 1)
                scalars_of(*after)
                sums_before(*nxt)
                split_squares(*prev, 1)
                mask(b, u, 1, 2)
                mask(b, u, 1, 3)
                clip_log(*nxt)
                split_squares(*prev, 2)
                refine_rstd(*after)
                decays(*nxt)
                chunk_out(b, u, 1)
                split_squares(*prev, 3)
                xt_low(*after)
                scale_y(*prev)

            set_up()
            for u in range(NU):
                slot(0, u)
            with dve.Fori(1, B - 1) as b:
                for u in range(NU):
                    slot(b, u)
            for u in range(NU):
                slot(B - 1, u)
            slot(B, 0)

        @block.tensor
        def _(pe):
            mm = nc.tensor.matmul

            def head_products():
                pe.wait_ge(heads_loaded, 16 * 3)
                pe.wait_ge(setup_v, V_ROW_MAX)
                mm(score_bank[0][:, 0:2 * KT], same_head_sb, row_max[:].rearrange("p w t -> p (w t)"),
                   start=True, stop=True).then_inc(setup_pe, 1)
                pe.wait_ge(setup_v, V_SW_DIAG)
                for i in range(2 * KT):
                    col = head_inv[:, i // KT, i % KT:i % KT + 1]
                    mm(hid_bank[0][:, i * P:i * P + P], col.to_broadcast([P, P]), ident_sb, start=True, stop=True)
                for m in range(KT):
                    for t in range(KT):
                        mm(hid_bank[1][:, m * H:m * H + H], qk_nat[:, 1, t, m * P:m * P + P], sw_diag[:, t],
                           start=(t == 0), stop=(t == KT - 1))
                for t in range(KT):
                    mm(score_bank[1][:, 0:H], head_un[:, t:t + 1].to_broadcast([P, P]), head_of_sb[:, t],
                       start=(t == 0), stop=(t == KT - 1))
                pe.wait_ge(tokens_w_loaded, 16 * 2)
                mm(score_bank[0][0:RANK, 0:D], fbt_sb, v_sb, start=True, stop=True).then_inc(setup_pe, 1)

            def fc_weights(i):
                t, g = i // 2, i % 2
                for j in range(4):
                    mm(fc_banks[i][:, j * P:j * P + P], fc_nat[:, 4 * g + j, t * P:t * P + P], fc_diag[:, 4 * g + j],
                       start=(j == 0), stop=False, skip_group_check=True)
                mm(fc_banks[i][:], fbv[:, t * P:t * P + P], ut_sb[:, 512 * g:512 * g + 512],
                   start=False, stop=True, skip_group_check=True).then_inc(ffn_fill, 1)

            def proj_weights(i):
                for j in range(2):
                    for o in range(KT):
                        last = nc.tensor.transpose(proj_banks[i][:, j * D + o * P:j * D + o * P + P],
                                                   pj_nat[:, o, (2 * i + j) * P:(2 * i + j) * P + P], ident_sb)
                last.then_inc(ffn_fill, 1)

            def proj_scale_row():
                for o in range(KT):
                    last = mm(y_bank[:, o * P:o * P + P], pj_scale[:, 0, o:o + 1].to_broadcast([P, P]), ident_sb,
                              start=True, stop=True)
                last.then_inc(ffn_fill, 1)

            def set_up():
                first, second = (0, 0), (0, 1)
                head_products()
                tokens_t(*first)
                pe.wait_ge(setup_v, V_WTOK)
                project(*first, 0)
                project(*first, 1)
                pe.wait_ge(fc_diag_done, 1)
                pe.wait_ge(setup_v, V_FC_TERNARY)
                fc_weights(0)
                fc_weights(1)
                stack_keys(*first, 0)
                stack_queries(*first, 0)
                fc_weights(2)
                fc_weights(3)
                cumulate(*first)
                queries_t(*first)
                pe.wait_ge(setup_v, V_PJ_TERNARY)
                proj_weights(0)
                proj_weights(1)
                stack_keys(*first, 1)
                pe.wait_ge(setup_v, V_FC_LOW - 1)
                proj_weights(2)
                proj_weights(3)
                stack_queries(*first, 1)
                proj_scale_row()
                decay_rows(*first)
                tokens_t(*second)
                pe.wait_ge(ffn_h_done, 8)
                pe.wait_ge(setup_v, V_FC_LOW)

            def tokens_t(b, u):
                if not exists(b):
                    return
                pb, pu = unit_after(b, u, -1)
                if exists(pb):
                    pe.wait_ge(q_diag_done, upto(pb, pu, 2 * CH, 3))
                for c in range(CH):
                    pe.wait_ge(xn_done, upto(b, u, CH, c))
                    for t in range(KT):
                        at = (c * KT + t) * P
                        last = nc.tensor.transpose(front_a[:, at:at + P], xn[:, u % 2, c, t * P:t * P + P], ident_sb)
                last.then_inc(front_full, 1)

            def token_product(bank, u, c, cols, width):
                n = 0
                for t in range(KT):
                    for lhs, rhs in ((xt_h, wtok_h), (xt_h, wtok_l), (xt_l, wtok_h)):
                        last = mm(bank[:, 0:width], lhs[:, u, c, t], rhs[:, t, cols:cols + width],
                                  start=(n == 0), stop=(n == 3 * KT - 1))
                        n += 1
                return last

            def project(b, u, c):
                if not exists(b):
                    return
                pe.wait_ge(xt_l_done, upto(b, u, 1, 0))
                if c == 0:
                    pb, pu = unit_after(b, u, -1)
                    if exists(pb):
                        pe.wait_ge(decay_t_done, upto(pb, pu, 1, 0))
                else:
                    pe.wait_ge(part_h_done, upto(b, u, CH, 0))
                token_product(front_b, u, c, 0, 2 * D).then_inc(front_full, 1)
                if c == 1:
                    pe.wait_ge(vg_done, upto(b, u, CH, 0))
                token_product(front_a, u, c, 2 * D, VG).then_inc(front_full, 1)

            def stack_keys(b, u, c):
                if not exists(b):
                    return
                bank = front_b[:].bitcast(F16)
                pe.wait_ge(parts_done, upto(b, u, CH, c))
                if c == 0:
                    pe.wait_ge(part_h_done, upto(b, u, CH, 1))
                else:
                    pe.wait_ge(q_t_done, upto(b, u, 1, 0))
                for g in range(PAIRS):
                    last = nc.tensor.transpose(bank[:, g * P:g * P + P],
                                               parts[:, c, H + 2 * g:H + 2 * g + 2].rearrange("p h s e -> p (h s e)"),
                                               ident16[:])
                last.then_inc(front_full, 1)

            def stack_queries(b, u, c):
                if not exists(b):
                    return
                bank = front_a[:].bitcast(F16)
                if c == 0:
                    pe.wait_ge(vg_done, upto(b, u, CH, 1))
                else:
                    pe.wait_ge(log_c_done, upto(b, u, 1, 0))
                for g in range(PAIRS):
                    last = nc.tensor.transpose(bank[:, g * P:g * P + P],
                                               parts[:, c, 2 * g:2 * g + 2].rearrange("p h s e -> p (h s e)"),
                                               ident16[:])
                last.then_inc(front_full, 1)

            def queries_t(b, u):
                if not exists(b):
                    return
                pe.wait_ge(k_stack_done, upto(b, u, CH, 0))
                for c in range(CH):
                    for t in range(KT):
                        at = (c * KT + t) * P
                        last = nc.tensor.transpose(front_b[:, at:at + P], qk[:, u % 2, c, t * P:t * P + P], ident_sb)
                last.then_inc(front_full, 1)

            def cumulate(b, u):
                if not exists(b):
                    return
                pe.wait_ge(q_diag_done, upto(b, u, 2 * CH, 1))
                pe.wait_ge(before_step, upto(b, u, 2, 0))
                cum = front_a[:, 0:CH * H]
                mm(cum, causal_sb, log_den[:].rearrange("p c h -> p (c h)"), start=True, stop=False)
                mm(cum, ones[:], before[:, u % 2].rearrange("p c h -> p (c h)"),
                   start=False, stop=True).then_inc(front_full, 1)

            def decay_rows(b, u):
                if not exists(b):
                    return
                pe.wait_ge(k_stack_done, upto(b, u, CH, 1))
                pe.wait_ge(decay_rep_done, upto(b, u, 1, 0))
                for c in range(CH):
                    for t in range(KT):
                        at = (c * KT + t) * P
                        last = nc.tensor.transpose(front_b[:, at:at + P], decay_rep[:, c, t * P:t * P + P], ident_sb)
                last.then_inc(front_full, 1)

            def scores(b, u, c, g):
                if not exists(b):
                    return
                par = u % 2
                pe.wait_ge(k_stack_done, upto(b, u, CH, c))
                pe.wait_ge(q_diag_done, upto(b, u, 2 * CH, 2 * c + 1))
                if started(upto(b, u, 4 * CH, 4 * c + g) - 2):
                    pe.wait_ge(mask_done, upto(b, u, 4 * CH, 4 * c + g) - 2)
                for i in range(2):
                    last = mm(score_bank[g % 2][:, i * 2 * P:(i + 1) * 2 * P], k_stack[:, par, c, 2 * g + i],
                              q_diag[:, par, c, 2 * g + i].rearrange("p s n -> p (s n)"), start=True, stop=True)
                last.then_inc(score_full, 1)

            def state_update(b, u, c):
                if not exists(b):
                    return
                par = u % 2
                pe.wait_ge(v_pad_done, upto(b, u, CH, c))
                if started(upto(b, u, CH, c) - 1):
                    pe.wait_ge(attn_done, upto(b, u, CH, c) - 1)
                for t in range(KT):
                    mm(attn_bank[:, (2 + t) * P:(3 + t) * P], qk[:, par, c, D + t * P:D + t * P + P],
                       v_heads(par, c, t * H // KT, H // KT), start=(t == 0), stop=False, skip_group_check=True)

            def values(b, u, c, half):
                if not exists(b):
                    return
                par = u % 2
                pe.wait_ge(mask_done, upto(b, u, 4 * CH, 4 * c + 2 * half + 1))
                for odd in range(2):
                    for q in range(4):
                        h = 2 * q + odd
                        last = mm(attn_bank[32 * q:32 * q + 32, half * P:half * P + P], v_pad[:, par, c, 8 * half + h],
                                  masked[:, 2 * half + h // 4, (h % 4) * P:(h % 4 + 1) * P],
                                  start=False, stop=False, skip_group_check=True)
                last.then_inc(values_done, 1)

            def carried(b, u, c):
                if not exists(b):
                    return
                pe.wait_ge(q_t_done, upto(b, u, 1, 0))
                if started(upto(b, u, CH, c) - 1):
                    pe.wait_ge(state_diag_done, upto(b, u, CH, c) - 1)
                for t in range(KT):
                    last = mm(attn_bank[:, t * P:t * P + P], state_diag[:, t], q_t[:, u % 2, c, t],
                              start=False, stop=True, skip_group_check=True)
                last.then_inc(attn_full, 1)

            def hidden(b, u, q):
                if not exists(b):
                    return
                bank = hid_bank[q % 2]
                if started(upto(b, u, 4, q) - 2):
                    pe.wait_ge(relu_done, upto(b, u, 4, q) - 2)
                for i in range(2):
                    j = 2 * q + i
                    n = 0
                    for t in range(KT):
                        for lhs, rhs in ((wfc_h, xt_h), (wfc_h, xt_l), (wfc_l, xt_h)):
                            last = mm(bank[:, i * UNIT:(i + 1) * UNIT], lhs[:, t, j * P:j * P + P], rhs[:, u, :, t],
                                      start=(n == 0), stop=(n == 3 * KT - 1))
                            n += 1
                last.then_inc(hid_full, 1)

            def projected(b, u, q):
                if not exists(b):
                    return
                if q == 0:
                    pb, pu = unit_after(b, u, -1)
                    if exists(pb):
                        pe.wait_ge(y_scaled_done, upto(pb, pu, 1, 0))
                pe.wait_ge(sq_l_done, upto(b, u, 4, q))
                for i in range(2):
                    for c in range(CH):
                        for n, part in enumerate((sq_h, sq_l)):
                            at = i * UNIT + c * P
                            last = mm(y_bank[:, c * D:(c + 1) * D], part[:, q, at:at + P], wproj_t[:, 2 * q + i],
                                      start=(q == i == c == n == 0), stop=False, skip_group_check=True)
                last.then_inc(proj_done, 1)

            def attn_projected(b, u):
                if not exists(b):
                    return
                par = u % 2
                pe.wait_ge(attn_l_done, upto(b, u, CH, CH - 1))
                for c in range(CH):
                    for t in range(KT):
                        for lhs, rhs in ((attn_h, wo_h), (attn_h, wo_l), (attn_l, wo_h)):
                            last = mm(y_bank[:, c * D:(c + 1) * D], lhs[:, par, c, t], rhs[:, t],
                                      start=False, stop=True, skip_group_check=True)
                last.then_inc(y_full, 1)

            def slot(b, u):
                nxt, prev, after = unit_after(b, u, 1), unit_after(b, u, -1), unit_after(b, u, 2)
                scores(b, u, 0, 0)
                scores(b, u, 0, 1)
                project(*nxt, 0)
                scores(b, u, 0, 2)
                scores(b, u, 0, 3)
                hidden(*prev, 0)
                state_update(b, u, 0)
                values(b, u, 0, 0)
                project(*nxt, 1)
                values(b, u, 0, 1)
                carried(b, u, 0)
                stack_keys(*nxt, 0)
                stack_queries(*nxt, 0)
                hidden(*prev, 1)
                scores(b, u, 1, 0)
                scores(b, u, 1, 1)
                projected(*prev, 0)
                hidden(*prev, 2)
                scores(b, u, 1, 2)
                scores(b, u, 1, 3)
                state_update(b, u, 1)
                cumulate(*nxt)
                values(b, u, 1, 0)
                projected(*prev, 1)
                queries_t(*nxt)
                hidden(*prev, 3)
                stack_keys(*nxt, 1)
                values(b, u, 1, 1)
                carried(b, u, 1)
                stack_queries(*nxt, 1)
                projected(*prev, 2)
                decay_rows(*nxt)
                projected(*prev, 3)
                tokens_t(*after)
                attn_projected(*prev)

            set_up()
            for u in range(NU):
                if u == 1:
                    pe.wait_ge(setup_v, V_DONE)
                slot(0, u)
            with pe.Fori(1, B - 1) as b:
                for u in range(NU):
                    slot(b, u)
            for u in range(NU):
                slot(B - 1, u)
            slot(B, 0)


def kernel(**inputs):
    import concourse.bacc as _bacc
    from concourse.bass_utils import run_bass_kernel_spmd as _run

    a = {k: np.asarray(v) for k, v in inputs.items()}
    heads = np.arange(D) // HD
    arrays = {
        "x": a["L0_attn_x"],
        "w_qk": np.stack([a["L0_attn_Wq"], a["L0_attn_Wk"]]),
        "w_qkv_t": np.concatenate([a[f"L0_attn_W{w}"].T for w in "qkv"], axis=1),
        "wo_t": a["L0_attn_Wo"].T,
        "gates": np.stack([np.tile(a[f"L0_attn_{w}w"].reshape(HD), H).reshape(KT, P).T for w in "gs"]),
        "low_rank": np.concatenate([a["L0_ffn_fast_b"].T, a["L0_ffn_v"], a["L0_ffn_u"].T,
                                    np.broadcast_to(a["L0_ffn_gate"].reshape(1, 1), (RANK, 1))], axis=1),
        "w_fc": a["L0_ffn_w_fc"], "w_proj": a["L0_ffn_w_proj"],
        "shapes": np.concatenate([np.eye(P), np.triu(np.ones((P, P))), heads[:P, None] == heads[None, :P],
                                  (heads[:, None] == np.arange(H)).reshape(KT, P, H).transpose(1, 0, 2).reshape(P, KT * H)],
                                 axis=1).astype(np.float32),
    }
    arrays = {f"in_{k}": np.ascontiguousarray(v) for k, v in arrays.items()}
    nc = _bacc.Bacc("TRN2", target_bir_lowering=False, num_devices=1)
    args = [nc.dram_tensor(k, v.shape, mybir.dt.from_np(v.dtype), kind="ExternalInput").ap() for k, v in arrays.items()]
    out = nc.dram_tensor("out_y", (B, L, D), F32, kind="ExternalOutput").ap()
    gated_attention_ternary_ffn(nc, *args, out)
    r = _run(nc, [arrays], core_ids=[0])
    return r.results[0]["out_y"]
```

```python
from contextlib import ExitStack

import numpy as np

import concourse.bass as bass
from concourse import mybir

F32 = mybir.dt.float32
F32R = mybir.dt.float32r
F16 = mybir.dt.float16
I32 = mybir.dt.int32
ALU = mybir.AluOpType
ACT = mybir.ActivationFunctionType
AX = mybir.AxisListType

P = 128
B, L, D = 8, 1024, 256
H, HD = 16, 16
HID = 1024
RANK = 16
KT = D // P
HT = HID // P
UNIT = 256
CH = UNIT // P
NU = L // UNIT
PAIRS = H // 2
LOGITS = D + RANK
VG = LOGITS + 2 * H
WTOK = 2 * D + VG
EPS = 1e-5

(XT, QK0, VG0, QK1, VG1, KS0, QS0, CUM, QT, KS1, QS1, GCT) = range(12)
FILLS = 12
FRONT_A = (XT, VG0, VG1, CUM, QS0, QS1)


def unit_after(b, u, k):
    return b + (u + k) // NU, (u + k) % NU


def exists(b):
    return not isinstance(b, int) or 0 <= b < B


def upto(b, u, per_unit, k):
    return (b * NU + u) * per_unit + k + 1


def started(value):
    return not isinstance(value, int) or value > 0


def gated_attention_ternary_ffn(nc, x, w_qk, w_qkvz_t, wo_t, gates, low_rank, w_fc, w_proj, shapes, out):
    x_v = x.rearrange("b l d -> (b l) d").rearrange("(t c p) d -> t p c d", c=CH, p=P)
    out_v = out.rearrange("b l d -> (b l) d").rearrange("(t c p) d -> t p c d", c=CH, p=P)

    with ExitStack() as ctx:
        def sb(name, shape, dt=F32):
            return ctx.enter_context(nc.sbuf_tensor(name, shape, dt))

        def psum(name):
            return ctx.enter_context(nc.psum_tensor(name, [P, 512], F32))

        def sem(name):
            return ctx.enter_context(nc.semaphore(name))

        shapes_sb = sb("shapes_sb", [P, 3 * P + KT * H])
        ident_sb = shapes_sb[:, 0:P]
        causal_sb = shapes_sb[:, P:2 * P]
        same_head_sb = shapes_sb[:, 2 * P:3 * P]
        head_of_sb = shapes_sb[:, 3 * P:].rearrange("p (t h) -> p t h", t=KT)
        ident16 = sb("ident16", [P, P], F16)
        ones = sb("ones", [P, P])
        w_stage = sb("w_stage", [P, KT, WTOK])
        wtok_h = sb("wtok_h", [P, KT, WTOK], F32R)
        wtok_l = sb("wtok_l", [P, KT, WTOK], F32R)
        wo_stage = sb("wo_stage", [P, KT, D])
        wo_h = sb("wo_h", [P, KT, D], F32R)
        wo_l = sb("wo_l", [P, KT, D], F32R)
        wfc_t = sb("wfc_t", [P, KT, HID], F32R)
        rank_w = sb("rank_w", [P, HID], F32R)
        wproj_t = sb("wproj_t", [P, HT, D], F32R)
        proj_scale = sb("proj_scale", [P, D])
        unscale = sb("unscale", [P, H])
        row_max = sb("row_max", [P, 2, KT])
        head_pow = sb("head_pow", [P, 2, KT])
        head_inv = sb("head_inv", [P, 2, KT])
        head_un = sb("head_un", [P, KT])
        gates_sb = sb("gates_sb", [P, 3, KT])
        gw_col, sw_col, rank_gate = gates_sb[:, 0], gates_sb[:, 1], gates_sb[:, 2, 0:1]
        sw_diag = sb("sw_diag", [P, KT, H])
        low_rank_sb = sb("low_rank_sb", [RANK, 3 * RANK + HID])
        fb_sb = low_rank_sb[:, 0:3 * RANK]
        ut_sb = low_rank_sb[:, 3 * RANK:]
        fc_inv = sb("fc_inv", [P, HT])
        rank_scale = sb("rank_scale", [P, HT])
        fc_scale = sb("fc_scale", [P, 3, HT])
        pj_scale = sb("pj_scale", [P, 3, KT])
        inv_proj = sb("inv_proj", [P, D])
        x_sb = sb("x_sb", [P, NU, CH, D])
        stats = sb("stats", [P, CH, 6])
        moments = sb("moments", [P, 2, CH, 2])
        neg_mean = sb("neg_mean", [P, 2, CH])
        var_eps = sb("var_eps", [P, 2, CH])
        log_var = sb("log_var", [P, 2, CH])
        guess = sb("guess", [P, 2, CH])
        newton = sb("newton", [P, 2, CH, 2])
        rstd = sb("rstd", [P, 2, CH])
        xn = sb("xn", [P, 2, CH, D])
        xt_h = sb("xt_h", [P, NU, CH, KT, P], F32R)
        z3 = sb("z3", [P, CH, P])
        z_stack = sb("z_stack", [P, NU, CH * P], F32R)
        xt_l = sb("xt_l", [P, NU, CH, KT, P], F32R)
        qk = sb("qk", [P, 2, CH, 2 * D])
        vg = sb("vg", [P, 2, CH, VG])
        parts = sb("parts", [P, CH, 2 * H, 4, HD], F16)
        k_stack = sb("k_stack", [P, 2, CH, PAIRS, P], F16)
        q_diag = sb("q_diag", [P, 2, CH, PAIRS, 2, P], F16)
        q_t = sb("q_t", [P, 2, CH, KT, P])
        exp_neg = sb("exp_neg", [P, CH, 2 * H])
        gate_den = sb("gate_den", [P, CH, H])
        write_den = sb("write_den", [P, CH, H])
        log_den = sb("log_den", [P, CH, H])
        before = sb("before", [P, 2, CH, H])
        log_c = sb("log_c", [P, CH, H])
        decay = sb("decay", [P, CH, H])
        write_full = sb("write_full", [P, CH, H])
        write_rec = sb("write_rec", [P, CH, H])
        write = sb("write", [P, 2, CH, H])
        decay_out = sb("decay_out", [P, CH, H])
        decay_rep = sb("decay_rep", [P, CH, D])
        decay_t = sb("decay_t", [P, 2, CH, KT, P])
        v_pad = sb("v_pad", [P, 2, CH, H, 2 * HD])
        masked = sb("masked", [P, 4, 512])
        state = sb("state", [P, KT, P])
        state_diag = sb("state_diag", [P, KT, P])
        attn = sb("attn", [P, CH, KT, P])
        attn_h = sb("attn_h", [P, 2, CH, KT, P], F32R)
        attn_l = sb("attn_l", [P, 2, CH, KT, P], F32R)
        relu_sq = sb("relu_sq", [P, 4, 512])
        relu, sq = relu_sq[:, 0:2], relu_sq[:, 2:4]
        sq_h = sb("sq_h", [P, 4, 512], F32R)
        sq_l = sb("sq_l", [P, 4, 512], F32R)
        y_both = sb("y_both", [P, 4, CH, D])
        y_scaled, y_out = y_both[:, 0:2], y_both[:, 2:4]
        fc_nat = relu_sq[:].rearrange("p g n -> p (g n)").rearrange("p (t n) -> p t n", t=HT)
        pj_nat = masked[:].rearrange("p g n -> p (g n)").rearrange("p (t n) -> p t n", t=KT)
        qk_nat = y_both[:, 0:2]
        fc_below = k_stack[:, 1].rearrange("p c g n -> p (c g n)").rearrange("p (t n) -> p t n", t=HT)
        spare = y_both[:, 2:4].rearrange("p g c n -> p (g c n)").bitcast(F16)
        fc_abs = spare.rearrange("p (t n) -> p t n", t=HT)
        pj_below = spare.rearrange("p (t n) -> p t n", t=KT)
        rank_nat = y_both[:, 0:2].rearrange("p g c n -> p (g c n)").rearrange("p (t n) -> p t n", t=HT)

        front_a = psum("front_a")
        front_b = psum("front_b")
        score_bank = [psum("score_a"), psum("score_b")]
        attn_bank = psum("attn_bank")
        hid_bank = [psum("hid_a"), psum("hid_b")]
        y_bank = psum("y_bank")

        z3_done = sem("z3_done")
        z_h_done = sem("z_h_done")
        z_l_done = sem("z_l_done")
        x_loaded = [sem(f"x_loaded{i}") for i in range(NU)]
        heads_loaded = sem("heads_loaded")
        tokens_w_loaded = sem("tokens_w_loaded")
        fc_loaded = sem("fc_loaded")
        proj_loaded = sem("proj_loaded")
        wo_loaded = sem("wo_loaded")
        zeroed = sem("zeroed")
        setup_v = sem("setup_v")
        setup_pe = sem("setup_pe")
        abs_sums_done = sem("abs_sums_done")
        below_done = sem("below_done")
        wtok_h_done = sem("wtok_h_done")
        ffn_fill = sem("ffn_fill")
        ffn_taken = sem("ffn_taken")
        stats_done = sem("stats_done")
        moments_done = sem("moments_done")
        ln_ready = sem("ln_ready")
        log_var_done = sem("log_var_done")
        guess_done = sem("guess_done")
        newton_step = sem("newton_step")
        rstd_done = sem("rstd_done")
        xn_done = sem("xn_done")
        front_full = sem("front_full")
        xt_h_done = sem("xt_h_done")
        xt_l_done = sem("xt_l_done")
        qk_done = sem("qk_done")
        vg_done = sem("vg_done")
        part_h_done = sem("part_h_done")
        part_l_done = sem("part_l_done")
        parts_done = sem("parts_done")
        k_stack_done = sem("k_stack_done")
        q_diag_done = sem("q_diag_done")
        q_t_done = sem("q_t_done")
        exp_neg_done = sem("exp_neg_done")
        dens_done = sem("dens_done")
        log_den_done = sem("log_den_done")
        before_step = sem("before_step")
        log_c_done = sem("log_c_done")
        decay_done = sem("decay_done")
        write_step = sem("write_step")
        write_done = sem("write_done")
        decay_out_done = sem("decay_out_done")
        decay_rep_done = sem("decay_rep_done")
        decay_t_done = sem("decay_t_done")
        v_pad_done = sem("v_pad_done")
        score_full = sem("score_full")
        mask_done = sem("mask_done")
        values_done = sem("values_done")
        attn_full = sem("attn_full")
        attn_done = sem("attn_done")
        state_done = sem("state_done")
        state_diag_done = sem("state_diag_done")
        attn_h_done = sem("attn_h_done")
        attn_l_done = sem("attn_l_done")
        hid_full = sem("hid_full")
        relu_done = sem("relu_done")
        sq_done = sem("sq_done")
        sq_h_done = sem("sq_h_done")
        sq_l_done = sem("sq_l_done")
        proj_done = sem("proj_done")
        y_full = sem("y_full")
        y_scaled_done = sem("y_scaled_done")
        y_out_done = sem("y_out_done")
        stored = [sem("stored_even"), sem("stored_odd")]

        V_ROW_MAX, V_HEAD_SCALES, V_SW_DIAG, V_FC_SCALES, V_FC_INV, V_W_STAGE, V_PJ_SCALES, V_WTOK = (
            1, 5, 6, 8, 10, 12, 15, 17)
        V_RANK_NAT, V_FC_TERNARY, V_PJ_TERNARY, V_RANK_LOW, V_DONE = 19, 20, 21, 23, 28
        PE_HEAD_SUM, PE_SMALL, PE_RANK = 1, 2, 3
        fc_banks = [hid_bank[0], hid_bank[1], y_bank, attn_bank]
        proj_banks = [*score_bank, *hid_bank]
        FC_FILL, RANK_FILL, PROJ_FILL, SCALE_ROW_FILL, FFN_FILLS = (0, 3, 4, 5), (1, 2), (6, 7, 9, 10), 8, 11

        def heads_bc(ap, n):
            return ap.unsqueeze(len(ap.shape)).to_broadcast([*ap.shape, n])

        def v_heads(par, c, first, count):
            flat = v_pad[:, par, c].rearrange("p h x -> p (h x)")[:, first * 2 * HD:(first + count) * 2 * HD]
            return flat.rearrange("p (g s e) -> p g s e", s=4, e=HD)[:, :, 0:4:3, :]

        block = ctx.enter_context(nc.Block())

        @block.sync
        def _(sp):
            def load(b, u):
                if not exists(b):
                    return
                if started(upto(b, u, 1, 0) - NU):
                    sp.wait_ge(y_out_done, upto(b, u, 1, 0) - NU)
                sp.dma_start(x_sb[:, u], x_v[b * NU + u]).then_inc(x_loaded[u], 16)

            def store(b, u):
                if not exists(b):
                    return
                sp.wait_ge(y_out_done, upto(b, u, 1, 0))
                sp.dma_start(out_v[b * NU + u], y_out[:, u % 2]).then_inc(stored[u % 2], 16)

            def slot(b, u):
                load(*unit_after(b, u, 3))
                store(*unit_after(b, u, -1))

            load(0, 0)
            sp.dma_start(shapes_sb[:], shapes).then_inc(heads_loaded, 16)
            sp.dma_start(w_stage[:, :, 0:2 * D + LOGITS], w_qkvz_t.rearrange("(t p) n -> p t n", p=P)).then_inc(tokens_w_loaded, 16)
            sp.dma_start(low_rank_sb[:], low_rank).then_inc(tokens_w_loaded, 16)
            sp.dma_start(wo_stage[:], wo_t.rearrange("(t p) n -> p t n", p=P)).then_inc(wo_loaded, 16)
            load(0, 1)
            load(0, 2)
            for u in range(NU):
                slot(0, u)
            with sp.Fori(1, B - 1) as b:
                for u in range(NU):
                    slot(b, u)
            for u in range(NU):
                slot(B - 1, u)
            slot(B, 0)
            for par in range(2):
                sp.wait_ge(stored[par], 16 * B * NU // 2)

        @block.gpsimd
        def _(pool):
            def waits_to_normalise(b, u):
                if not exists(b):
                    return
                pool.wait_ge(rstd_done, upto(b, u, 1, 0))
                if started(upto(b, u, FILLS, XT) - 2 * FILLS):
                    pool.wait_ge(front_full, upto(b, u, FILLS, XT) - 2 * FILLS)

            def normalise(b, u):
                if not exists(b):
                    return
                for c in range(CH):
                    nc.gpsimd.tensor_scalar(xn[:, u % 2, c], x_sb[:, u, c], neg_mean[:, u % 2, c:c + 1],
                                            rstd[:, u % 2, c:c + 1], ALU.add, ALU.mult).then_inc(xn_done, 1)

            def repeat_z(b, u):
                if not exists(b):
                    return
                pool.wait_ge(vg_done, upto(b, u, CH, CH - 1))
                if started(upto(b, u, FILLS, CUM) - FILLS):
                    pool.wait_ge(front_full, upto(b, u, FILLS, CUM) - FILLS)
                nc.gpsimd.tensor_tensor(z3[:, :, 0:3 * RANK].rearrange("p c (s k) -> p c s k", s=3),
                                        vg[:, u % 2, :, D:LOGITS].unsqueeze(2).to_broadcast([P, CH, 3, RANK]),
                                        ones[:, 0:CH * 3 * RANK].rearrange("p (c s k) -> p c s k", c=CH, s=3),
                                        ALU.mult).then_inc(z3_done, 1)

            def values_and_decay(b, u):
                if not exists(b):
                    return
                par = u % 2
                pool.wait_ge(write_done, upto(b, u, 1, 0))
                pool.wait_ge(vg_done, upto(b, u, CH, CH - 1))
                pb, pu = unit_after(b, u, -2)
                if exists(pb):
                    pool.wait_ge(attn_full, upto(pb, pu, CH, CH - 1))
                for c in range(CH):
                    if c == CH - 1:
                        pool.wait_ge(decay_out_done, upto(b, u, 1, 0))
                        if started(upto(b, u, FILLS, GCT) - FILLS):
                            pool.wait_ge(front_full, upto(b, u, FILLS, GCT) - FILLS)
                    val = vg[:, par, c, 0:D].rearrange("p (g s e) -> p g s e", s=2, e=HD)
                    fac = heads_bc(write[:, par, c], HD).rearrange("p (g s) e -> p g s e", s=2)
                    nc.gpsimd.tensor_tensor(v_heads(par, c, 0, H), val, fac, ALU.mult).then_inc(v_pad_done, 1)
                nc.gpsimd.tensor_scalar(decay_rep[:].rearrange("p c (h e) -> p (c h) e", e=HD),
                                        heads_bc(decay_out[:].rearrange("p c h -> p (c h)"), HD), 1.0, 1.0,
                                        ALU.mult, ALU.mult).then_inc(decay_rep_done, 1)

            def diagonal_state(b, u, c):
                if not exists(b):
                    return
                pool.wait_ge(state_done, upto(b, u, CH, c))
                if (u, c) != (NU - 1, CH - 1):
                    nc.gpsimd.tensor_tensor(state_diag[:], state[:],
                                            same_head_sb.unsqueeze(1).to_broadcast([P, KT, P]),
                                            ALU.mult).then_inc(state_diag_done, 1)

            def attn_parts(b, u, c):
                if not exists(b):
                    return
                pb, pu = unit_after(b, u, -2)
                if exists(pb):
                    pool.wait_ge(y_full, upto(pb, pu, 1, 0))
                pool.wait_ge(attn_done, upto(b, u, CH, c))
                nc.gpsimd.tensor_tensor(attn_h[:, u % 2, c], attn[:, c], ones[:].unsqueeze(1).to_broadcast([P, KT, P]),
                                        ALU.mult).then_inc(attn_h_done, 1)
                pool.wait_ge(attn_h_done, upto(b, u, CH, c))
                nc.gpsimd.tensor_tensor(attn_l[:, u % 2, c], attn[:, c], attn_h[:, u % 2, c].bitcast(F32),
                                        ALU.subtract).then_inc(attn_l_done, 1)
                if (u, c) == (NU - 1, CH - 1):
                    nc.gpsimd.memset(state_diag[:], 0.0).then_inc(state_diag_done, 1)

            def residual(b, u):
                if not exists(b):
                    return
                pool.wait_ge(y_scaled_done, upto(b, u, 1, 0))
                pb, pu = unit_after(b, u, -2)
                if exists(pb):
                    pool.wait_ge(stored[u % 2], (pb * (NU // 2) + pu // 2 + 1) * 16)
                nc.gpsimd.tensor_tensor(y_out[:, u % 2], y_scaled[:, u % 2], x_sb[:, u], ALU.add).then_inc(y_out_done, 1)

            def slot(b, u):
                nxt, prev, after = unit_after(b, u, 1), unit_after(b, u, -1), unit_after(b, u, 2)
                repeat_z(*nxt)
                diagonal_state(b, u, 0)
                attn_parts(b, u, 0)
                waits_to_normalise(*after)
                values_and_decay(*nxt)
                normalise(*after)
                diagonal_state(b, u, 1)
                attn_parts(b, u, 1)
                residual(*prev)

            def below(nat, tiles, scales, low):
                for t in range(tiles):
                    last = nc.gpsimd.tensor_scalar(low[:, t], nat[:, t], scales[:, 2, t:t + 1], None, ALU.is_lt)
                last.then_inc(below_done, 1)

            nc.gpsimd.memset(state_diag[:], 0.0).then_inc(zeroed, 1)
            nc.gpsimd.memset(ones[:], 1.0).then_inc(zeroed, 1)
            nc.gpsimd.memset(z3[:], 0.0).then_inc(zeroed, 1)
            waits_to_normalise(0, 0)
            normalise(0, 0)
            nc.gpsimd.memset(v_pad[:], 0.0).then_inc(zeroed, 1)
            nc.gpsimd.memset(q_diag[:], 0.0).then_inc(zeroed, 1)
            pool.wait_ge(setup_v, V_FC_SCALES)
            below(fc_nat, HT, fc_scale, fc_below)
            pool.wait_ge(setup_v, V_PJ_SCALES)
            below(pj_nat, KT, pj_scale, pj_below)
            pool.wait_ge(zeroed, 5)
            slot(-1, NU - 1)
            for u in range(NU):
                slot(0, u)
            with pool.Fori(1, B - 1) as b:
                for u in range(NU):
                    slot(b, u)
            for u in range(NU):
                slot(B - 1, u)
            slot(B, 0)

        @block.scalar
        def _(act):
            def filled(b, u, fill):
                act.wait_ge(front_full, upto(b, u, FILLS, fill))
                return front_a if fill in FRONT_A else front_b

            def rstd_guess(b, u):
                if not exists(b):
                    return
                par = u % 2
                act.wait_ge(ln_ready, upto(b, u, 1, 0))
                nc.scalar.activation(log_var[:, par], var_eps[:, par], ACT.Ln).then_inc(log_var_done, 1)
                act.wait_ge(log_var_done, upto(b, u, 1, 0))
                nc.scalar.activation(guess[:, par], log_var[:, par], ACT.Exp, scale=-0.5).then_inc(guess_done, 1)

            def xt_high(b, u):
                if not exists(b):
                    return
                bank = filled(b, u, XT)
                pb, pu = unit_after(b, u, -NU)
                if exists(pb):
                    act.wait_ge(hid_full, upto(pb, pu, 4, 3))
                nc.scalar.activation(xt_h[:, u], bank[:].rearrange("p (c t n) -> p c t n", c=CH, t=KT),
                                     ACT.Copy).then_inc(xt_h_done, 1)

            def projected(b, u, c):
                if not exists(b):
                    return
                par = u % 2
                bank = filled(b, u, [QK0, QK1][c])
                pb, pu = unit_after(b, u, -2)
                if exists(pb):
                    act.wait_ge(attn_full, upto(pb, pu, CH, CH - 1))
                    act.wait_ge(v_pad_done, upto(pb, pu, CH, CH - 1))
                nc.scalar.activation(qk[:, par, c], bank[:], ACT.Copy).then_inc(qk_done, 1)
                pb, pu = unit_after(b, u, -1)
                if exists(pb):
                    act.wait_ge(front_full, upto(pb, pu, FILLS, QS1))
                nc.scalar.activation(parts[:, c, :, 0, :], bank[:].rearrange("p (h e) -> p h e", e=HD),
                                     ACT.Copy).then_inc(part_h_done, 1)
                bank = filled(b, u, [VG0, VG1][c])
                nc.scalar.activation(vg[:, par, c], bank[:, 0:VG], ACT.Copy).then_inc(vg_done, 1)

            def gate_exp(b, u):
                if not exists(b):
                    return
                act.wait_ge(vg_done, upto(b, u, CH, CH - 1))
                pb, pu = unit_after(b, u, -1)
                if exists(pb):
                    act.wait_ge(dens_done, upto(pb, pu, 2, 1))
                nc.scalar.activation(exp_neg[:], vg[:, u % 2, :, LOGITS:VG], ACT.Exp, scale=-1.0).then_inc(exp_neg_done, 1)

            def gate_log(b, u):
                if not exists(b):
                    return
                act.wait_ge(dens_done, upto(b, u, 2, 1))
                pb, pu = unit_after(b, u, -1)
                if exists(pb):
                    act.wait_ge(front_full, upto(pb, pu, FILLS, CUM))
                    act.wait_ge(before_step, upto(pb, pu, 2, 1))
                nc.scalar.activation(log_den[:], gate_den[:], ACT.Ln).then_inc(log_den_done, 1)

            def keys_stacked(b, u, c):
                if not exists(b):
                    return
                bank = filled(b, u, [KS0, KS1][c])
                pb, pu = unit_after(b, u, -2)
                if exists(pb):
                    act.wait_ge(score_full, upto(pb, pu, 4 * CH, 4 * CH - 1))
                nc.scalar.activation(k_stack[:, u % 2, c], bank[:].bitcast(F16).rearrange("p (g n) -> p g n", g=PAIRS),
                                     ACT.Copy).then_inc(k_stack_done, 1)

            def queries_stacked(b, u, c):
                if not exists(b):
                    return
                bank = filled(b, u, [QS0, QS1][c])
                if isinstance(b, int) and b == 0 and u < 2:
                    act.wait_ge(zeroed, 5)
                for half in range(2):
                    rows = slice(64 * half, 64 * half + 64)
                    nc.scalar.activation(q_diag[rows, u % 2, c, :, half, :],
                                         bank[rows].bitcast(F16).rearrange("p (g n) -> p g n", g=PAIRS),
                                         ACT.Copy).then_inc(q_diag_done, 1)

            def z_high(b, u):
                if not exists(b):
                    return
                bank = filled(b, u, CUM)
                nc.scalar.activation(z_stack[:, u], bank[:, CH * H:CH * H + CH * P], ACT.Copy).then_inc(z_h_done, 1)

            def query_t(b, u):
                if not exists(b):
                    return
                bank = filled(b, u, QT)
                nc.scalar.activation(q_t[:, u % 2], bank[:].rearrange("p (c t n) -> p c t n", c=CH, t=KT),
                                     ACT.Copy).then_inc(q_t_done, 1)

            def decay_exp(b, u):
                if not exists(b):
                    return
                act.wait_ge(log_c_done, upto(b, u, 1, 0))
                pb, pu = unit_after(b, u, -1)
                if exists(pb):
                    act.wait_ge(decay_out_done, upto(pb, pu, 1, 0))
                nc.scalar.activation(decay[:], log_c[:], ACT.Exp, scale=-1.0).then_inc(decay_done, 1)

            def decay_transposed(b, u):
                if not exists(b):
                    return
                bank = filled(b, u, GCT)
                pb, pu = unit_after(b, u, -2)
                if exists(pb):
                    act.wait_ge(attn_done, upto(pb, pu, CH, CH - 1))
                nc.scalar.activation(decay_t[:, u % 2], bank[:].rearrange("p (c t n) -> p c t n", c=CH, t=KT),
                                     ACT.Copy).then_inc(decay_t_done, 1)

            def squares(b, u, q):
                if not exists(b):
                    return
                n = q % 2
                act.wait_ge(hid_full, upto(b, u, 4, q))
                nc.scalar.activation(relu[:, n], hid_bank[n][:], ACT.Relu).then_inc(relu_done, 1)
                if started(upto(b, u, 4, q) - 2):
                    act.wait_ge(sq_l_done, upto(b, u, 4, q) - 2)
                act.wait_ge(relu_done, upto(b, u, 4, q))
                for i in range(2):
                    half = slice(i * UNIT, (i + 1) * UNIT)
                    last = nc.scalar.activation(sq[:, n, half], relu[:, n, half], ACT.Square,
                                                scale=fc_scale[:, 0, 2 * q + i:2 * q + i + 1])
                last.then_inc(sq_done, 1)

            def slot(b, u):
                nxt, prev, after = unit_after(b, u, 1), unit_after(b, u, -1), unit_after(b, u, 2)
                projected(*nxt, 0)
                squares(*prev, 0)
                projected(*nxt, 1)
                gate_exp(*nxt)
                keys_stacked(*nxt, 0)
                gate_log(*nxt)
                queries_stacked(*nxt, 0)
                squares(*prev, 1)
                squares(*prev, 2)
                rstd_guess(*after)
                decay_exp(*nxt)
                z_high(*nxt)
                query_t(*nxt)
                squares(*prev, 3)
                keys_stacked(*nxt, 1)
                queries_stacked(*nxt, 1)
                decay_transposed(*nxt)
                xt_high(*after)

            def abs_sums(nat, tiles, scales, scratch):
                for t in range(tiles):
                    last = nc.scalar.activation(scratch[:, t], nat[:, t], ACT.Abs, accum_out=scales[:, 0, t:t + 1])
                last.then_inc(abs_sums_done, 1)

            def token_weights_high():
                for t in range(KT):
                    act.wait_ge(setup_v, V_W_STAGE - KT + 1 + t)
                    nc.scalar.activation(wtok_h[:, t], w_stage[:, t], ACT.Copy).then_inc(wtok_h_done, 1)

            def fc_taken(i):
                act.wait_ge(ffn_fill, FC_FILL[i] + 1)
                nc.scalar.activation(wfc_t[:, i // 2, 512 * (i % 2):512 * (i % 2) + 512], fc_banks[i][:],
                                     ACT.Copy).then_inc(ffn_taken, 1)

            def rank_high(i):
                act.wait_ge(ffn_fill, RANK_FILL[i] + 1)
                nc.scalar.activation(rank_w[:, 512 * i:512 * i + 512], score_bank[i][:], ACT.Copy).then_inc(ffn_taken, 1)

            def proj_taken(i):
                act.wait_ge(ffn_fill, PROJ_FILL[i] + 1)
                nc.scalar.activation(wproj_t[:, 2 * i:2 * i + 2, :], proj_banks[i][:].rearrange("p (t n) -> p t n", t=2),
                                     ACT.Copy).then_inc(ffn_taken, 1)

            def set_up():
                first, second = (0, 0), (0, 1)
                rstd_guess(*first)
                act.wait_ge(fc_loaded, 16)
                abs_sums(fc_nat, HT, fc_scale, fc_abs)
                act.wait_ge(proj_loaded, 16)
                act.wait_ge(abs_sums_done, 1)
                abs_sums(pj_nat, KT, pj_scale, pj_below)
                xt_high(*first)
                token_weights_high()
                projected(*first, 0)
                projected(*first, 1)
                gate_exp(*first)
                gate_log(*first)
                fc_taken(0)
                keys_stacked(*first, 0)
                queries_stacked(*first, 0)
                rank_high(0)
                rank_high(1)
                fc_taken(1)
                fc_taken(2)
                fc_taken(3)
                rstd_guess(*second)
                query_t(*first)
                decay_exp(*first)
                z_high(*first)
                proj_taken(0)
                keys_stacked(*first, 1)
                proj_taken(1)
                queries_stacked(*first, 1)
                decay_transposed(*first)
                xt_high(*second)
                proj_taken(2)
                proj_taken(3)

            act.dma_start(qk_nat, w_qk.rearrange("w (t p) n -> p w t n", p=P)).then_inc(heads_loaded, 16)
            act.dma_start(gates_sb[:], gates.rearrange("g p t -> p g t")).then_inc(heads_loaded, 16)
            act.dma_start(fc_nat, w_fc.rearrange("(t p) n -> p t n", p=P)).then_inc(fc_loaded, 16)
            act.dma_start(pj_nat, w_proj.rearrange("(t p) n -> p t n", p=P)).then_inc(proj_loaded, 16)
            nc.scalar.preload_act_table_set("natural_log_exp_and_others")
            set_up()
            for u in range(NU):
                slot(0, u)
            with act.Fori(1, B - 1) as b:
                for u in range(NU):
                    slot(b, u)
            for u in range(NU):
                slot(B - 1, u)
            slot(B, 0)

        @block.vector
        def _(dve):
            steps = [0]

            def count(ins):
                steps[0] += 1
                ins.then_inc(setup_v, 1)

            def step(ins):
                count(ins)
                dve.wait_ge(setup_v, steps[0])

            def head_scales():
                step(nc.vector.tensor_reduce(row_max[:].rearrange("p w t -> p (w t)"),
                                             qk_nat.rearrange("p w t n -> p (w t) n"), AX.X, ALU.max,
                                             apply_absolute_value=True))
                assert steps[0] == V_ROW_MAX
                dve.wait_ge(setup_pe, PE_HEAD_SUM)
                pow2 = head_pow[:].rearrange("p w t -> p (w t)")
                step(nc.vector.tensor_scalar(pow2, score_bank[0][:, 0:2 * KT], 1e-30, None, ALU.max))
                step(nc.vector.tensor_scalar(pow2.bitcast(I32), pow2.bitcast(I32), 0x7F800000, None, ALU.bitwise_and))
                step(nc.vector.reciprocal(head_inv[:].rearrange("p w t -> p (w t)"), pow2))
                count(nc.vector.tensor_tensor(head_un[:], head_pow[:, 0], head_pow[:, 1], ALU.mult))
                assert steps[0] == V_HEAD_SCALES
                nc.vector.tensor_scalar(sw_diag[:, 0], head_of_sb[:, 0], sw_col[:, 0:1], None, ALU.mult)
                count(nc.vector.tensor_scalar(sw_diag[:, 1], head_of_sb[:, 1], sw_col[:, 1:2], None, ALU.mult))
                assert steps[0] == V_SW_DIAG

            def token_weights():
                for t in range(KT):
                    nc.vector.tensor_scalar(w_stage[:, t, 2 * D + LOGITS:2 * D + LOGITS + H], head_of_sb[:, t], gw_col[:, t:t + 1], None,
                                            ALU.mult)
                dve.wait_ge(setup_pe, PE_SMALL)
                nc.vector.tensor_copy(w_stage[:, :, 2 * D + LOGITS + H:WTOK],
                                      hid_bank[1][:, 0:KT * H].rearrange("p (t h) -> p t h", t=KT))
                dve.wait_ge(tokens_w_loaded, 16 * 2)
                for t in range(KT):
                    cols = w_stage[:, t, 0:2 * D]
                    count(nc.vector.tensor_tensor(cols, cols, hid_bank[0][:], ALU.mult))
                assert steps[0] == V_W_STAGE
                count(nc.vector.tensor_scalar(unscale[:], score_bank[1][:, 0:H], 1.0 / HD, None, ALU.mult))

            def rank_weights():
                dve.wait_ge(setup_pe, PE_RANK)
                step(nc.vector.memset(rank_nat, 0.0))
                count(nc.vector.tensor_tensor(rank_nat[:, :, 0:3 * RANK],
                                              score_bank[0][:, 0:HT * 3 * RANK].rearrange("p (t k) -> p t k", t=HT),
                                              heads_bc(rank_scale[:], 3 * RANK), ALU.mult))
                assert steps[0] == V_RANK_NAT

            def scales_of(scales, width):
                step(nc.vector.tensor_scalar(scales[:, 0], scales[:, 0], 1.0 / width, 1e-5, ALU.mult, ALU.max))
                nc.vector.tensor_scalar(scales[:, 1], scales[:, 0], 0.5, None, ALU.mult)
                count(nc.vector.tensor_scalar(scales[:, 2], scales[:, 0], -0.5, None, ALU.mult))

            def ternary(nat, tiles, scales, low):
                for t in range(tiles):
                    last = nc.vector.scalar_tensor_tensor(out=nat[:, t], in0=nat[:, t], scalar=scales[:, 1, t:t + 1],
                                                          in1=low[:, t], op0=ALU.is_gt, op1=ALU.subtract)
                count(last)

            def rank_low(i):
                rows, cols = slice(2 * RANK, 3 * RANK), slice(512 * i, 512 * i + 512)
                dve.wait_ge(ffn_taken, RANK_FILL[i] + 1)
                count(nc.vector.tensor_tensor(rank_w[rows, cols], score_bank[i][rows], rank_w[rows, cols].bitcast(F32),
                                              ALU.subtract))

            def output_weights():
                dve.wait_ge(ffn_fill, SCALE_ROW_FILL + 1)
                step(nc.vector.tensor_copy(proj_scale[:], y_bank[:, 0:D]))
                step(nc.vector.reciprocal(inv_proj[:], proj_scale[:]))
                dve.wait_ge(wo_loaded, 16)
                step(nc.vector.tensor_tensor(wo_stage[:], wo_stage[:], inv_proj[:].unsqueeze(1).to_broadcast([P, KT, D]),
                                             ALU.mult))
                step(nc.vector.tensor_copy(wo_h[:], wo_stage[:]))
                count(nc.vector.tensor_tensor(wo_l[:], wo_stage[:], wo_h[:].bitcast(F32), ALU.subtract))
                assert steps[0] == V_DONE

            def set_up():
                first, second = (0, 0), (0, 1)
                nc.vector.memset(before[:], 0.0)
                stats_of(*first)
                waits_for_stats(*first)
                moments_of(*first)
                scalars_of(*first)
                refine_rstd(*first)
                dve.wait_ge(heads_loaded, 16 * 3)
                nc.vector.tensor_copy(ident16[:], ident_sb)
                head_scales()
                dve.wait_ge(abs_sums_done, 1)
                scales_of(fc_scale, D)
                assert steps[0] == V_FC_SCALES
                step(nc.vector.reciprocal(fc_inv[:], fc_scale[:, 0]))
                count(nc.vector.tensor_scalar(rank_scale[:], fc_inv[:], rank_gate, None, ALU.mult))
                assert steps[0] == V_FC_INV
                token_weights()
                dve.wait_ge(abs_sums_done, 2)
                scales_of(pj_scale, HID)
                assert steps[0] == V_PJ_SCALES
                xt_low(*first)
                for t in range(KT):
                    dve.wait_ge(wtok_h_done, t + 1)
                    count(nc.vector.tensor_tensor(wtok_l[:, t], w_stage[:, t], wtok_h[:, t].bitcast(F32), ALU.subtract))
                assert steps[0] == V_WTOK
                rank_weights()
                dve.wait_ge(below_done, 1)
                ternary(fc_nat, HT, fc_scale, fc_below)
                assert steps[0] == V_FC_TERNARY
                qk_parts(*first, 0)
                dens(*first)
                qk_parts(*first, 1)
                sums_before(*first)
                dve.wait_ge(below_done, 2)
                ternary(pj_nat, KT, pj_scale, pj_below)
                assert steps[0] == V_PJ_TERNARY
                stats_of(*second)
                waits_for_stats(*second)
                moments_of(*second)
                scalars_of(*second)
                rank_low(0)
                rank_low(1)
                assert steps[0] == V_RANK_LOW
                clip_log(*first)
                z_low(*first)
                refine_rstd(*second)
                decays(*first)
                output_weights()
                xt_low(*second)
                dve.wait_ge(ffn_fill, FFN_FILLS)

            def stats_of(b, u):
                if not exists(b):
                    return
                dve.wait_ge(x_loaded[u], (b + 1) * 16)
                for c in range(CH):
                    last = nc.vector.bn_stats(stats[:, c], x_sb[:, u, c])
                last.then_inc(stats_done, 1)

            def waits_for_stats(b, u):
                if not exists(b):
                    return
                dve.wait_ge(stats_done, upto(b, u, 1, 0))

            def moments_of(b, u):
                if not exists(b):
                    return
                for c in range(CH):
                    last = nc.vector.bn_aggr(moments[:, u % 2, c], stats[:, c])
                last.then_inc(moments_done, 1)

            def scalars_of(b, u):
                if not exists(b):
                    return
                par = u % 2
                pb, pu = unit_after(b, u, -2)
                if exists(pb):
                    dve.wait_ge(xn_done, upto(pb, pu, CH, CH - 1))
                dve.wait_ge(moments_done, upto(b, u, 1, 0))
                nc.vector.tensor_scalar(neg_mean[:, par], moments[:, par, :, 0], -1.0, None, ALU.mult)
                nc.vector.tensor_scalar(var_eps[:, par], moments[:, par, :, 1], EPS, None, ALU.add).then_inc(ln_ready, 1)

            def refine_rstd(b, u):
                if not exists(b):
                    return
                par = u % 2
                y, a = guess[:, par], var_eps[:, par]
                sqr, corr = newton[:, par, :, 0], newton[:, par, :, 1]
                dve.wait_ge(guess_done, upto(b, u, 1, 0))
                dve.wait_ge(ln_ready, upto(b, u, 1, 0))
                nc.vector.tensor_tensor(sqr, y, y, ALU.mult).then_inc(newton_step, 1)
                dve.wait_ge(newton_step, upto(b, u, 2, 0))
                nc.vector.scalar_tensor_tensor(out=corr, in0=sqr, scalar=-0.5, in1=a, op0=ALU.mult,
                                               op1=ALU.mult).then_inc(newton_step, 1)
                dve.wait_ge(newton_step, upto(b, u, 2, 1))
                nc.vector.scalar_tensor_tensor(out=rstd[:, par], in0=corr, scalar=1.5, in1=y, op0=ALU.add,
                                               op1=ALU.mult).then_inc(rstd_done, 1)

            def xt_low(b, u):
                if not exists(b):
                    return
                dve.wait_ge(xt_h_done, upto(b, u, 1, 0))
                nc.vector.tensor_tensor(xt_l[:, u], front_a[:].rearrange("p (c t n) -> p c t n", c=CH, t=KT),
                                        xt_h[:, u].bitcast(F32), ALU.subtract).then_inc(xt_l_done, 1)

            def qk_parts(b, u, c):
                if not exists(b):
                    return
                src = qk[:, u % 2, c].rearrange("p (h e) -> p h e", e=HD)
                dve.wait_ge(part_h_done, upto(b, u, CH, c))
                nc.vector.tensor_tensor(parts[:, c, :, 2, :], src, parts[:, c, :, 0, :],
                                        ALU.subtract).then_inc(part_l_done, 1)
                dve.wait_ge(part_l_done, upto(b, u, CH, c))
                q, k = parts[:, c, 0:H], parts[:, c, H:2 * H]
                nc.vector.tensor_copy(q[:, :, 1::2, :], q[:, :, 0::2, :])
                nc.vector.tensor_copy(k[:, :, 3, :], k[:, :, 0, :])
                nc.vector.tensor_copy(k[:, :, 1, :], k[:, :, 2, :]).then_inc(parts_done, 1)

            def dens(b, u):
                if not exists(b):
                    return
                dve.wait_ge(exp_neg_done, upto(b, u, 1, 0))
                pb, pu = unit_after(b, u, -1)
                if exists(pb):
                    dve.wait_ge(log_den_done, upto(pb, pu, 1, 0))
                nc.vector.tensor_scalar(gate_den[:], exp_neg[:, :, 0:H], 1.0, 1e6, ALU.add, ALU.min).then_inc(dens_done, 1)
                nc.vector.tensor_scalar(write_den[:], exp_neg[:, :, H:2 * H], 1.0, None, ALU.add).then_inc(dens_done, 1)

            def sums_before(b, u):
                if not exists(b):
                    return
                par = u % 2
                dve.wait_ge(log_den_done, upto(b, u, 1, 0))
                if started(upto(b, u, 2, 0) - 1):
                    dve.wait_ge(before_step, upto(b, u, 2, 0) - 1)
                nc.vector.tensor_tensor(before[:, par, 1], before[:, par, 0], log_den[:, 0], ALU.add).then_inc(before_step, 1)
                dve.wait_ge(before_step, upto(b, u, 2, 0))
                if u == NU - 1:
                    nc.vector.memset(before[:, 1 - par, 0], 0.0).then_inc(before_step, 1)
                else:
                    nc.vector.tensor_tensor(before[:, 1 - par, 0], before[:, par, 1], log_den[:, 1],
                                            ALU.add).then_inc(before_step, 1)

            def clip_log(b, u):
                if not exists(b):
                    return
                dve.wait_ge(front_full, upto(b, u, FILLS, CUM))
                pb, pu = unit_after(b, u, -1)
                if exists(pb):
                    dve.wait_ge(decay_done, upto(pb, pu, 1, 0))
                nc.vector.tensor_scalar(log_c[:], front_a[:, 0:CH * H].rearrange("p (c h) -> p c h", c=CH), 30.0, -30.0,
                                        ALU.min, ALU.max).then_inc(log_c_done, 1)

            def z_low(b, u):
                if not exists(b):
                    return
                dve.wait_ge(z_h_done, upto(b, u, 1, 0))
                nc.vector.tensor_tensor(z_stack[0:RANK, u], front_a[0:RANK, CH * H:CH * H + CH * P],
                                        z_stack[0:RANK, u].bitcast(F32), ALU.subtract).then_inc(z_l_done, 1)

            def decays(b, u):
                if not exists(b):
                    return
                par = u % 2
                dve.wait_ge(decay_done, upto(b, u, 1, 0))
                nc.vector.scalar_tensor_tensor(out=write_full[:], in0=decay[:], scalar=1e-6, in1=write_den[:],
                                               op0=ALU.add, op1=ALU.mult).then_inc(write_step, 1)
                dve.wait_ge(write_step, upto(b, u, 2, 0))
                nc.vector.reciprocal(write_rec[:], write_full[:]).then_inc(write_step, 1)
                pb, pu = unit_after(b, u, -2)
                if exists(pb):
                    dve.wait_ge(v_pad_done, upto(pb, pu, CH, CH - 1))
                dve.wait_ge(write_step, upto(b, u, 2, 1))
                nc.vector.tensor_tensor(write[:, par], write_rec[:], vg[:, par, :, LOGITS + H:VG], ALU.mult).then_inc(write_done, 1)
                pb, pu = unit_after(b, u, -1)
                if exists(pb):
                    dve.wait_ge(decay_rep_done, upto(pb, pu, 1, 0))
                nc.vector.scalar_tensor_tensor(out=decay_out[:], in0=decay[:], scalar=1e-6,
                                               in1=unscale[:].unsqueeze(1).to_broadcast([P, CH, H]),
                                               op0=ALU.add, op1=ALU.mult).then_inc(decay_out_done, 1)

            def mask(b, u, c, g):
                if not exists(b):
                    return
                dve.wait_ge(score_full, upto(b, u, 4 * CH, 4 * c + g))
                if started(upto(b, u, 2 * CH, 2 * c + g // 2) - 2):
                    dve.wait_ge(values_done, upto(b, u, 2 * CH, 2 * c + g // 2) - 2)
                nc.vector.tensor_tensor(masked[:, g].rearrange("p (h n) -> p h n", h=4),
                                        score_bank[g % 2][:].rearrange("p (h n) -> p h n", h=4),
                                        causal_sb.unsqueeze(1).to_broadcast([P, 4, P]), ALU.mult).then_inc(mask_done, 1)

            def chunk_out(b, u, c):
                if not exists(b):
                    return
                par = u % 2
                dve.wait_ge(attn_full, upto(b, u, CH, c))
                update = attn_bank[:, 2 * P:4 * P].rearrange("p (t n) -> p t n", t=KT)
                if started(upto(b, u, CH, c) - 1):
                    dve.wait_ge(state_diag_done, upto(b, u, CH, c) - 1)
                if (u, c) == (0, 0):
                    nc.vector.tensor_copy(state[:], update).then_inc(state_done, 1)
                else:
                    if started(upto(b, u, CH, c) - 1):
                        dve.wait_ge(state_done, upto(b, u, CH, c) - 1)
                    nc.vector.tensor_tensor(state[:], state[:], update, ALU.add).then_inc(state_done, 1)
                dve.wait_ge(decay_t_done, upto(b, u, 1, 0))
                pb, pu = unit_after(b, u, -1)
                if exists(pb):
                    dve.wait_ge(attn_l_done, upto(pb, pu, CH, c))
                nc.vector.tensor_tensor(attn[:, c], attn_bank[:, 0:2 * P].rearrange("p (t n) -> p t n", t=KT),
                                        decay_t[:, par, c], ALU.mult).then_inc(attn_done, 1)

            def split_squares(b, u, q):
                if not exists(b):
                    return
                n = q % 2
                dve.wait_ge(sq_done, upto(b, u, 4, q))
                if started(upto(b, u, 4, q) - 4):
                    dve.wait_ge(proj_done, upto(b, u, 4, q) - 4)
                nc.vector.tensor_copy(sq_h[:, q], sq[:, n]).then_inc(sq_h_done, 1)
                dve.wait_ge(sq_h_done, upto(b, u, 4, q))
                nc.vector.tensor_tensor(sq_l[:, q], sq[:, n], sq_h[:, q].bitcast(F32), ALU.subtract).then_inc(sq_l_done, 1)

            def scale_y(b, u):
                if not exists(b):
                    return
                dve.wait_ge(y_full, upto(b, u, 1, 0))
                pb, pu = unit_after(b, u, -2)
                if exists(pb):
                    dve.wait_ge(y_out_done, upto(pb, pu, 1, 0))
                nc.vector.tensor_tensor(y_scaled[:, u % 2], y_bank[:].rearrange("p (c n) -> p c n", c=CH),
                                        proj_scale[:].unsqueeze(1).to_broadcast([P, CH, D]),
                                        ALU.mult).then_inc(y_scaled_done, 1)

            def slot(b, u):
                nxt, prev, after = unit_after(b, u, 1), unit_after(b, u, -1), unit_after(b, u, 2)
                mask(b, u, 0, 0)
                mask(b, u, 0, 1)
                mask(b, u, 0, 2)
                mask(b, u, 0, 3)
                qk_parts(*nxt, 0)
                stats_of(*after)
                split_squares(*prev, 0)
                qk_parts(*nxt, 1)
                dens(*nxt)
                chunk_out(b, u, 0)
                waits_for_stats(*after)
                mask(b, u, 1, 0)
                moments_of(*after)
                mask(b, u, 1, 1)
                scalars_of(*after)
                sums_before(*nxt)
                split_squares(*prev, 1)
                mask(b, u, 1, 2)
                mask(b, u, 1, 3)
                clip_log(*nxt)
                refine_rstd(*after)
                decays(*nxt)
                z_low(*nxt)
                split_squares(*prev, 2)
                split_squares(*prev, 3)
                chunk_out(b, u, 1)
                xt_low(*after)
                scale_y(*prev)

            set_up()
            for u in range(NU):
                slot(0, u)
            with dve.Fori(1, B - 1) as b:
                for u in range(NU):
                    slot(b, u)
            for u in range(NU):
                slot(B - 1, u)
            slot(B, 0)

        @block.tensor
        def _(pe):
            mm = nc.tensor.matmul

            def head_products():
                pe.wait_ge(heads_loaded, 16 * 3)
                pe.wait_ge(setup_v, V_ROW_MAX)
                mm(score_bank[0][:, 0:2 * KT], same_head_sb, row_max[:].rearrange("p w t -> p (w t)"),
                   start=True, stop=True).then_inc(setup_pe, 1)
                tokens_t(0, 0)
                pe.wait_ge(setup_v, V_SW_DIAG)
                for i in range(2 * KT):
                    col = head_inv[:, i // KT, i % KT:i % KT + 1]
                    mm(hid_bank[0][:, i * P:i * P + P], col.to_broadcast([P, P]), ident_sb, start=True, stop=True)
                for m in range(KT):
                    for t in range(KT):
                        mm(hid_bank[1][:, m * H:m * H + H], qk_nat[:, 1, t, m * P:m * P + P], sw_diag[:, t],
                           start=(t == 0), stop=(t == KT - 1))
                for t in range(KT):
                    last = mm(score_bank[1][:, 0:H], head_un[:, t:t + 1].to_broadcast([P, P]), head_of_sb[:, t],
                              start=(t == 0), stop=(t == KT - 1))
                last.then_inc(setup_pe, 1)
                pe.wait_ge(tokens_w_loaded, 16 * 2)
                for j in range(HT):
                    last = mm(score_bank[0][:, j * 3 * RANK:(j + 1) * 3 * RANK], ut_sb[:, j * P:j * P + P], fb_sb,
                              start=True, stop=True)
                last.then_inc(setup_pe, 1)

            def fc_weights(i):
                for j in range(4):
                    last = nc.tensor.transpose(fc_banks[i][:, j * P:j * P + P],
                                               fc_nat[:, 4 * (i % 2) + j, (i // 2) * P:(i // 2 + 1) * P], ident_sb)
                last.then_inc(ffn_fill, 1)

            def rank_weights(i):
                for j in range(4):
                    last = nc.tensor.transpose(score_bank[i][:, j * P:j * P + P], rank_nat[:, 4 * i + j], ident_sb)
                last.then_inc(ffn_fill, 1)

            def proj_weights(i):
                for j in range(2):
                    for o in range(KT):
                        last = nc.tensor.transpose(proj_banks[i][:, j * D + o * P:j * D + o * P + P],
                                                   pj_nat[:, o, (2 * i + j) * P:(2 * i + j) * P + P], ident_sb)
                last.then_inc(ffn_fill, 1)

            def proj_scale_row():
                for o in range(KT):
                    last = mm(y_bank[:, o * P:o * P + P], pj_scale[:, 0, o:o + 1].to_broadcast([P, P]), ident_sb,
                              start=True, stop=True)
                last.then_inc(ffn_fill, 1)

            def set_up():
                first, second = (0, 0), (0, 1)
                head_products()
                pe.wait_ge(setup_v, V_WTOK)
                project(*first, 0)
                project(*first, 1)
                pe.wait_ge(setup_v, V_FC_TERNARY)
                fc_weights(0)
                stack_keys(*first, 0)
                stack_queries(*first, 0)
                rank_weights(0)
                rank_weights(1)
                fc_weights(1)
                fc_weights(2)
                fc_weights(3)
                cumulate(*first)
                queries_t(*first)
                pe.wait_ge(setup_v, V_RANK_LOW)
                proj_weights(0)
                stack_keys(*first, 1)
                proj_weights(1)
                pe.wait_ge(ffn_taken, FC_FILL[2] + 1)
                proj_scale_row()
                stack_queries(*first, 1)
                decay_rows(*first)
                tokens_t(*second)
                proj_weights(2)
                proj_weights(3)
                pe.wait_ge(ffn_taken, PROJ_FILL[1] + 1)

            def tokens_t(b, u):
                if not exists(b):
                    return
                pb, pu = unit_after(b, u, -1)
                if exists(pb):
                    pe.wait_ge(q_diag_done, upto(pb, pu, 2 * CH, 3))
                for c in range(CH):
                    pe.wait_ge(xn_done, upto(b, u, CH, c))
                    for t in range(KT):
                        at = (c * KT + t) * P
                        last = nc.tensor.transpose(front_a[:, at:at + P], xn[:, u % 2, c, t * P:t * P + P], ident_sb)
                last.then_inc(front_full, 1)

            def token_product(bank, u, c, cols, width):
                n = 0
                for t in range(KT):
                    for lhs, rhs in ((xt_h, wtok_h), (xt_h, wtok_l), (xt_l, wtok_h)):
                        last = mm(bank[:, 0:width], lhs[:, u, c, t], rhs[:, t, cols:cols + width],
                                  start=(n == 0), stop=(n == 3 * KT - 1))
                        n += 1
                return last

            def project(b, u, c):
                if not exists(b):
                    return
                pe.wait_ge(xt_l_done, upto(b, u, 1, 0))
                if c == 0:
                    pb, pu = unit_after(b, u, -1)
                    if exists(pb):
                        pe.wait_ge(decay_t_done, upto(pb, pu, 1, 0))
                else:
                    pe.wait_ge(part_h_done, upto(b, u, CH, 0))
                token_product(front_b, u, c, 0, 2 * D).then_inc(front_full, 1)
                if c == 1:
                    pe.wait_ge(vg_done, upto(b, u, CH, 0))
                token_product(front_a, u, c, 2 * D, VG).then_inc(front_full, 1)

            def stack_keys(b, u, c):
                if not exists(b):
                    return
                bank = front_b[:].bitcast(F16)
                pe.wait_ge(parts_done, upto(b, u, CH, c))
                if c == 0:
                    pe.wait_ge(part_h_done, upto(b, u, CH, 1))
                else:
                    pe.wait_ge(q_t_done, upto(b, u, 1, 0))
                for g in range(PAIRS):
                    last = nc.tensor.transpose(bank[:, g * P:g * P + P],
                                               parts[:, c, H + 2 * g:H + 2 * g + 2].rearrange("p h s e -> p (h s e)"),
                                               ident16[:])
                last.then_inc(front_full, 1)

            def stack_queries(b, u, c):
                if not exists(b):
                    return
                bank = front_a[:].bitcast(F16)
                if c == 0:
                    pe.wait_ge(vg_done, upto(b, u, CH, 1))
                else:
                    pe.wait_ge(log_c_done, upto(b, u, 1, 0))
                    pe.wait_ge(z_l_done, upto(b, u, 1, 0))
                for g in range(PAIRS):
                    last = nc.tensor.transpose(bank[:, g * P:g * P + P],
                                               parts[:, c, 2 * g:2 * g + 2].rearrange("p h s e -> p (h s e)"),
                                               ident16[:])
                last.then_inc(front_full, 1)

            def queries_t(b, u):
                if not exists(b):
                    return
                pe.wait_ge(k_stack_done, upto(b, u, CH, 0))
                for c in range(CH):
                    for t in range(KT):
                        at = (c * KT + t) * P
                        last = nc.tensor.transpose(front_b[:, at:at + P], qk[:, u % 2, c, t * P:t * P + P], ident_sb)
                last.then_inc(front_full, 1)

            def cumulate(b, u):
                if not exists(b):
                    return
                pe.wait_ge(q_diag_done, upto(b, u, 2 * CH, 1))
                pe.wait_ge(before_step, upto(b, u, 2, 0))
                cum = front_a[:, 0:CH * H]
                mm(cum, causal_sb, log_den[:].rearrange("p c h -> p (c h)"), start=True, stop=False)
                mm(cum, ones[:], before[:, u % 2].rearrange("p c h -> p (c h)"), start=False, stop=True)
                pe.wait_ge(z3_done, upto(b, u, 1, 0))
                for c in range(CH):
                    last = nc.tensor.transpose(front_a[:, CH * H + c * P:CH * H + c * P + P], z3[:, c], ident_sb)
                last.then_inc(front_full, 1)

            def decay_rows(b, u):
                if not exists(b):
                    return
                pe.wait_ge(k_stack_done, upto(b, u, CH, 1))
                pe.wait_ge(decay_rep_done, upto(b, u, 1, 0))
                for c in range(CH):
                    for t in range(KT):
                        at = (c * KT + t) * P
                        last = nc.tensor.transpose(front_b[:, at:at + P], decay_rep[:, c, t * P:t * P + P], ident_sb)
                last.then_inc(front_full, 1)

            def scores(b, u, c, g):
                if not exists(b):
                    return
                par = u % 2
                pe.wait_ge(k_stack_done, upto(b, u, CH, c))
                pe.wait_ge(q_diag_done, upto(b, u, 2 * CH, 2 * c + 1))
                if started(upto(b, u, 4 * CH, 4 * c + g) - 2):
                    pe.wait_ge(mask_done, upto(b, u, 4 * CH, 4 * c + g) - 2)
                for i in range(2):
                    last = mm(score_bank[g % 2][:, i * 2 * P:(i + 1) * 2 * P], k_stack[:, par, c, 2 * g + i],
                              q_diag[:, par, c, 2 * g + i].rearrange("p s n -> p (s n)"), start=True, stop=True)
                last.then_inc(score_full, 1)

            def state_update(b, u, c):
                if not exists(b):
                    return
                par = u % 2
                pe.wait_ge(v_pad_done, upto(b, u, CH, c))
                if started(upto(b, u, CH, c) - 1):
                    pe.wait_ge(attn_done, upto(b, u, CH, c) - 1)
                for t in range(KT):
                    mm(attn_bank[:, (2 + t) * P:(3 + t) * P], qk[:, par, c, D + t * P:D + t * P + P],
                       v_heads(par, c, t * H // KT, H // KT), start=(t == 0), stop=False, skip_group_check=True)

            def values(b, u, c, half):
                if not exists(b):
                    return
                par = u % 2
                pe.wait_ge(mask_done, upto(b, u, 4 * CH, 4 * c + 2 * half + 1))
                for odd in range(2):
                    for q in range(4):
                        h = 2 * q + odd
                        last = mm(attn_bank[32 * q:32 * q + 32, half * P:half * P + P], v_pad[:, par, c, 8 * half + h],
                                  masked[:, 2 * half + h // 4, (h % 4) * P:(h % 4 + 1) * P],
                                  start=False, stop=False, skip_group_check=True)
                last.then_inc(values_done, 1)

            def carried(b, u, c):
                if not exists(b):
                    return
                pe.wait_ge(q_t_done, upto(b, u, 1, 0))
                if started(upto(b, u, CH, c) - 1):
                    pe.wait_ge(state_diag_done, upto(b, u, CH, c) - 1)
                for t in range(KT):
                    last = mm(attn_bank[:, t * P:t * P + P], state_diag[:, t], q_t[:, u % 2, c, t],
                              start=False, stop=True, skip_group_check=True)
                last.then_inc(attn_full, 1)

            def hidden(b, u, q):
                if not exists(b):
                    return
                bank = hid_bank[q % 2]
                if started(upto(b, u, 4, q) - 2):
                    pe.wait_ge(relu_done, upto(b, u, 4, q) - 2)
                pe.wait_ge(z_l_done, upto(b, u, 1, 0))
                for i in range(2):
                    j = 2 * q + i
                    place = bank[:, i * UNIT:(i + 1) * UNIT]
                    for t in range(KT):
                        for part in (xt_h, xt_l):
                            mm(place, wfc_t[:, t, j * P:j * P + P], part[:, u, :, t],
                               start=(t == 0 and part is xt_h), stop=False)
                    last = mm(place, rank_w[:, j * P:j * P + P], z_stack[:, u], start=False, stop=True)
                last.then_inc(hid_full, 1)

            def projected(b, u, q):
                if not exists(b):
                    return
                if q == 0:
                    pb, pu = unit_after(b, u, -1)
                    if exists(pb):
                        pe.wait_ge(y_scaled_done, upto(pb, pu, 1, 0))
                pe.wait_ge(sq_l_done, upto(b, u, 4, q))
                for i in range(2):
                    for c in range(CH):
                        for n, part in enumerate((sq_h, sq_l)):
                            at = i * UNIT + c * P
                            last = mm(y_bank[:, c * D:(c + 1) * D], part[:, q, at:at + P], wproj_t[:, 2 * q + i],
                                      start=(q == i == c == n == 0), stop=False, skip_group_check=True)
                last.then_inc(proj_done, 1)

            def attn_projected(b, u):
                if not exists(b):
                    return
                par = u % 2
                pe.wait_ge(attn_l_done, upto(b, u, CH, CH - 1))
                for c in range(CH):
                    for t in range(KT):
                        for lhs, rhs in ((attn_h, wo_h), (attn_h, wo_l), (attn_l, wo_h)):
                            last = mm(y_bank[:, c * D:(c + 1) * D], lhs[:, par, c, t], rhs[:, t],
                                      start=False, stop=True, skip_group_check=True)
                last.then_inc(y_full, 1)

            def slot(b, u):
                nxt, prev, after = unit_after(b, u, 1), unit_after(b, u, -1), unit_after(b, u, 2)
                scores(b, u, 0, 0)
                scores(b, u, 0, 1)
                project(*nxt, 0)
                scores(b, u, 0, 2)
                scores(b, u, 0, 3)
                hidden(*prev, 0)
                state_update(b, u, 0)
                values(b, u, 0, 0)
                project(*nxt, 1)
                values(b, u, 0, 1)
                carried(b, u, 0)
                stack_keys(*nxt, 0)
                stack_queries(*nxt, 0)
                hidden(*prev, 1)
                scores(b, u, 1, 0)
                scores(b, u, 1, 1)
                projected(*prev, 0)
                hidden(*prev, 2)
                scores(b, u, 1, 2)
                scores(b, u, 1, 3)
                state_update(b, u, 1)
                cumulate(*nxt)
                queries_t(*nxt)
                values(b, u, 1, 0)
                hidden(*prev, 3)
                projected(*prev, 1)
                stack_keys(*nxt, 1)
                values(b, u, 1, 1)
                carried(b, u, 1)
                stack_queries(*nxt, 1)
                projected(*prev, 2)
                decay_rows(*nxt)
                projected(*prev, 3)
                tokens_t(*after)
                attn_projected(*prev)

            set_up()
            for u in range(NU):
                if u == 1:
                    pe.wait_ge(setup_v, V_DONE)
                    pe.wait_ge(ffn_taken, FFN_FILLS - 1)
                slot(0, u)
            with pe.Fori(1, B - 1) as b:
                for u in range(NU):
                    slot(b, u)
            for u in range(NU):
                slot(B - 1, u)
            last = (B - 1, NU - 1)
            hidden(*last, 0)
            hidden(*last, 1)
            hidden(*last, 2)
            projected(*last, 0)
            hidden(*last, 3)
            projected(*last, 1)
            projected(*last, 2)
            projected(*last, 3)
            attn_projected(*last)


def kernel(**inputs):
    import concourse.bacc as _bacc
    from concourse.bass_utils import run_bass_kernel_spmd as _run

    a = {k: np.asarray(v) for k, v in inputs.items()}
    heads = np.arange(D) // HD
    arrays = {
        "x": a["L0_attn_x"],
        "w_qk": np.stack([a["L0_attn_Wq"], a["L0_attn_Wk"]]),
        "w_qkvz_t": np.concatenate([*(a[f"L0_attn_W{w}"].T for w in "qkv"), a["L0_ffn_v"].T], axis=1),
        "wo_t": a["L0_attn_Wo"].T,
        "gates": np.stack([*(np.tile(a[f"L0_attn_{w}w"].reshape(HD), H).reshape(KT, P).T for w in "gs"),
                           np.broadcast_to(a["L0_ffn_gate"].reshape(1, 1), (P, KT))]),
        "low_rank": np.concatenate([*[a["L0_ffn_fast_b"]] * 3, a["L0_ffn_u"].T], axis=1),
        "w_fc": a["L0_ffn_w_fc"], "w_proj": a["L0_ffn_w_proj"],
        "shapes": np.concatenate([np.eye(P), np.triu(np.ones((P, P))), heads[:P, None] == heads[None, :P],
                                  (heads[:, None] == np.arange(H)).reshape(KT, P, H).transpose(1, 0, 2).reshape(P, KT * H)],
                                 axis=1).astype(np.float32),
    }
    arrays = {f"in_{k}": np.ascontiguousarray(v) for k, v in arrays.items()}
    nc = _bacc.Bacc("TRN2", target_bir_lowering=False, num_devices=1)
    args = [nc.dram_tensor(k, v.shape, mybir.dt.from_np(v.dtype), kind="ExternalInput").ap() for k, v in arrays.items()]
    out = nc.dram_tensor("out_y", (B, L, D), F32, kind="ExternalOutput").ap()
    gated_attention_ternary_ffn(nc, *args, out)
    r = _run(nc, [arrays], core_ids=[0])
    return r.results[0]["out_y"]
```
